# Optimizing a Trainium2 kernel written in Bass

```python
import numpy as np
import jax
import jax.numpy as jnp

def _softmax(x, axis=-1):
    return jax.nn.softmax(x, axis=axis)

def _gelu(x):
    return jax.nn.gelu(x, approximate=True)

def _silu(x):
    return jax.nn.silu(x)

def _sigmoid(x):
    return jax.nn.sigmoid(x)

def _layernorm(x, axis=-1, eps=1e-05):
    m = jnp.mean(x, axis=axis, keepdims=True)
    v = jnp.var(x, axis=axis, keepdims=True)
    return (x - m) / jnp.sqrt(v + eps)

def _scatter_add(tgt, idx, src, axis=0):
    return tgt.at[idx].add(src)

def _segment_sum(src, seg, n):
    return jax.ops.segment_sum(src, seg, n)
kernel_name = 'mk_gnn_resnorm_d2_gnn_r8_782bdf'

def setup_inputs(seed: int=0):
    np.random.seed(seed)
    _w = jnp.asarray

    def _rec_inputs():
        import jax
        import jax.numpy as jnp
        _gk = jax.random.key(seed)
        x = -0.0003713 + 1 * jax.random.normal(jax.random.fold_in(_gk, 1), (6250, 256), jnp.float32)
        _s = jax.random.randint(jax.random.fold_in(_gk, 2), (50000,), 0, 6250, jnp.int32)
        _d = jax.random.randint(jax.random.fold_in(_gk, 3), (50000,), 0, 6250, jnp.int32)
        _loop = jnp.arange(6250, dtype=jnp.int32)
        src = jnp.concatenate([_s, _d, _loop])
        dst = jnp.concatenate([_d, _s, _loop])
        _o = jnp.argsort(dst, stable=True)
        src = src[_o]
        dst = dst[_o]
        edge_attr_3 = 0.000857669 + 1.0001 * jax.random.normal(jax.random.fold_in(_gk, 12), (106250, 3), jnp.float32)
        edge_attr_50 = 2.43349e-05 + 1.00019 * jax.random.normal(jax.random.fold_in(_gk, 13), (106250, 50), jnp.float32)
        edge_type_16 = jax.random.randint(jax.random.fold_in(_gk, 15), (106250,), 0, 16, jnp.int32)
        edge_weight1 = jax.random.uniform(jax.random.fold_in(_gk, 16), (106250, 1), jnp.float32, 0.0, 1)
        return (x, src, dst, edge_attr_3, edge_attr_50, edge_type_16, edge_weight1)
    x, src, dst, edge_attr_3, edge_attr_50, edge_type_16, edge_weight1 = _rec_inputs()

    def _L0_gnn_setup():
        import jax, jax.numpy as jnp
        import numpy as np
        N = 6250
        E = 100000
        IN = 256
        OUT = 256
        R = 16
        B = 8
        key = jax.random.key(seed)
        ks = jax.random.split(key, 8)
        feat = jax.random.normal(ks[0], (N, IN), dtype=jnp.float32)
        norm = jax.random.uniform(ks[1], (E, 1), dtype=jnp.float32)
        w_scale = np.sqrt(2.0 / (IN + OUT)).astype(np.float32)
        weight = jax.random.normal(ks[2], (B, IN, OUT), dtype=jnp.float32) * w_scale
        w_comp = jax.random.normal(ks[3], (R, B), dtype=jnp.float32) * np.float32(np.sqrt(2.0 / (R + B)))
        h_bias = jnp.zeros((OUT,), dtype=jnp.float32)
        loop_weight = jax.random.normal(ks[4], (IN, OUT), dtype=jnp.float32) * w_scale
        src = jax.random.randint(ks[5], (E,), 0, N)
        dst = jax.random.randint(ks[6], (E,), 0, N)
        etypes = jax.random.randint(ks[7], (E,), 0, R)
        return {'feat': feat, 'norm': norm, 'weight': weight, 'w_comp': w_comp, 'h_bias': h_bias, 'loop_weight': loop_weight, 'src': src, 'dst': dst, 'etypes': etypes}
    _L0_gnn_all = _L0_gnn_setup()
    _L0_gnn_in = {k: v for k, v in _L0_gnn_all.items() if k in ('weight', 'w_comp', 'h_bias', 'loop_weight')}
    del _L0_gnn_all

    def _L1_gnn_setup():
        import jax, jax.numpy as jnp
        import numpy as np
        CUTOFF = 2.0
        LOG2 = float(np.log(2.0))

        def ssp(x):
            return jax.nn.softplus(x) - LOG2
        key = jax.random.key(seed)
        ks = jax.random.split(key, 12)
        N, E, H, F, G = (1250, 40000, 256, 256, 50)
        x = jax.random.normal(ks[0], (N, H), dtype=jnp.float32)
        edge_index = jax.random.randint(ks[1], (2, E), 0, N, dtype=jnp.int64)
        edge_weight = jax.random.normal(ks[2], (E, 3), dtype=jnp.float32)
        edge_attr = jax.random.normal(ks[3], (E, G), dtype=jnp.float32)
        s = lambda fan_in: 1.0 / np.sqrt(fan_in)
        mlp_w1 = jax.random.uniform(ks[4], (G, F), jnp.float32, -s(G), s(G))
        mlp_b1 = jax.random.uniform(ks[5], (F,), jnp.float32, -s(G), s(G))
        mlp_w2 = jax.random.uniform(ks[6], (F, F), jnp.float32, -s(F), s(F))
        mlp_b2 = jax.random.uniform(ks[7], (F,), jnp.float32, -s(F), s(F))
        lin1_w = jax.random.uniform(ks[8], (H, F), jnp.float32, -s(H), s(H))
        lin2_w = jax.random.uniform(ks[9], (F, H), jnp.float32, -s(F), s(F))
        lin2_b = jax.random.uniform(ks[10], (H,), jnp.float32, -s(F), s(F))
        return {'x': x, 'edge_index': edge_index, 'edge_weight': edge_weight, 'edge_attr': edge_attr, 'mlp_w1': mlp_w1, 'mlp_b1': mlp_b1, 'mlp_w2': mlp_w2, 'mlp_b2': mlp_b2, 'lin1_w': lin1_w, 'lin2_w': lin2_w, 'lin2_b': lin2_b}
    _L1_gnn_all = _L1_gnn_setup()
    _L1_gnn_in = {k: v for k, v in _L1_gnn_all.items() if k in ('mlp_w1', 'mlp_b1', 'mlp_w2', 'mlp_b2', 'lin1_w', 'lin2_w', 'lin2_b')}
    del _L1_gnn_all
    return {'x': x, 'src': src, 'dst': dst, 'edge_attr_3': edge_attr_3, 'edge_attr_50': edge_attr_50, 'edge_type_16': edge_type_16, 'edge_weight1': edge_weight1, 'L0_gnn_weight': _L0_gnn_in['weight'], 'L0_gnn_w_comp': _L0_gnn_in['w_comp'], 'L0_gnn_h_bias': _L0_gnn_in['h_bias'], 'L0_gnn_loop_weight': _L0_gnn_in['loop_weight'], 'L1_gnn_mlp_w1': _L1_gnn_in['mlp_w1'], 'L1_gnn_mlp_b1': _L1_gnn_in['mlp_b1'], 'L1_gnn_mlp_w2': _L1_gnn_in['mlp_w2'], 'L1_gnn_mlp_b2': _L1_gnn_in['mlp_b2'], 'L1_gnn_lin1_w': _L1_gnn_in['lin1_w'], 'L1_gnn_lin2_w': _L1_gnn_in['lin2_w'], 'L1_gnn_lin2_b': _L1_gnn_in['lin2_b']}

def reference(x, src, dst, edge_attr_3, edge_attr_50, edge_type_16, edge_weight1, L0_gnn_weight, L0_gnn_w_comp, L0_gnn_h_bias, L0_gnn_loop_weight, L1_gnn_mlp_w1, L1_gnn_mlp_b1, L1_gnn_mlp_w2, L1_gnn_mlp_b2, L1_gnn_lin1_w, L1_gnn_lin2_w, L1_gnn_lin2_b):
    import jax
    import jax.numpy as jnp

    def _L0_gnn_ref(feat, norm, weight, w_comp, h_bias, loop_weight, src, dst, etypes):
        import jax, jax.numpy as jnp
        import numpy as np
        N = 6250
        E = 100000
        IN = 256
        OUT = 256
        R = 16
        B = 8
        w_full = jnp.einsum('rb,bdo->rdo', w_comp, weight)
        x_rel = jnp.einsum('nd,rdo->rno', feat, w_full)
        msg = x_rel[etypes, src] * norm
        agg = jax.ops.segment_sum(msg, dst, num_segments=N)
        out = agg + h_bias + feat @ loop_weight
        return jax.nn.relu(out)

    def _L1_gnn_ref(x, edge_index, edge_weight, edge_attr, mlp_w1, mlp_b1, mlp_w2, mlp_b2, lin1_w, lin2_w, lin2_b):
        import jax, jax.numpy as jnp
        import numpy as np
        CUTOFF = 2.0
        LOG2 = float(np.log(2.0))

        def ssp(x):
            return jax.nn.softplus(x) - LOG2
        N = x.shape[0]
        distances = jnp.linalg.norm(edge_weight, axis=1)
        C = 0.5 * (jnp.cos(distances * jnp.pi / CUTOFF) + 1.0)
        C = C * (distances <= CUTOFF)
        W = ssp(edge_attr @ mlp_w1 + mlp_b1) @ mlp_w2 + mlp_b2
        W = W * C[:, None]
        i, j = (edge_index[0], edge_index[1])
        messages = W * (x[j] @ lin1_w)
        agg = jax.ops.segment_sum(messages, i, num_segments=N)
        h = ssp(agg @ lin2_w + lin2_b)
        return x + h
    edge_index = jnp.stack([src, dst])
    x = _layernorm(x + _L0_gnn_ref(x, edge_weight1, L0_gnn_weight, L0_gnn_w_comp, L0_gnn_h_bias, L0_gnn_loop_weight, src, dst, edge_type_16), axis=-1)
    x = _layernorm(x + _L1_gnn_ref(x, edge_index, edge_attr_3, edge_attr_50, L1_gnn_mlp_w1, L1_gnn_mlp_b1, L1_gnn_mlp_w2, L1_gnn_mlp_b2, L1_gnn_lin1_w, L1_gnn_lin2_w, L1_gnn_lin2_b), axis=-1)
    return x

_drawn_inputs = setup_inputs


def setup_inputs(seed=0):
    import zlib

    import numpy as np

    out = dict(_drawn_inputs(seed))
    spreads = {'L0_gnn_h_bias': (0.0, 0.1)}
    factors = {'edge_attr_3': 13.51,
     'L1_gnn_mlp_w1': 13.095,
     'L1_gnn_mlp_b1': 200.0,
     'L1_gnn_mlp_b2': 200.0,
     'L1_gnn_lin2_b': 6.037,
     'edge_attr_50': 4.881,
     'L1_gnn_mlp_w2': 4.399,
     'L1_gnn_lin1_w': 3.927,
     'L1_gnn_lin2_w': 3.914}
    for name, (base, spread) in spreads.items():
        noise = np.random.default_rng([zlib.crc32(name.encode()), seed]).standard_normal(out[name].shape)
        drawn = base * np.exp(spread * noise) if base else spread * noise
        out[name] = jnp.asarray(drawn.astype(out[name].dtype))
    for name, factor in factors.items():
        out[name] = (out[name] * factor).astype(out[name].dtype)
    return out
```

```python
import concourse.bass as bass
from concourse import mybir
from contextlib import ExitStack
import math

F32 = mybir.dt.float32
BF16 = mybir.dt.bfloat16
I32 = mybir.dt.int32
ALU = mybir.AluOpType
ACT = mybir.ActivationFunctionType
AXX = mybir.AxisListType.X

P = 128
N = 6250
D = 256
DK = D // P
E = 106250
REL = 16
BASES = 8
G50 = 50
NBLK = -(-N // P)
EC = -(-E // P) + 1
EP = P * EC
PADNODE = NBLK * P
META = 6
M_ROW, M_NORM, M_DST, M_SLOT, M_CUT, M_SRC = range(META)
MSG = D + 8

B_UNROLL = 16
TILES_D = -(-((E + NBLK * (P - 1)) // P) // B_UNROLL) * B_UNROLL
D_UNROLL = 8
PAIR = 2 * P
TILES_S = -(-((E + NBLK * (PAIR - 1)) // PAIR) // D_UNROLL) * D_UNROLL
CD = -(-TILES_D // P)
CS = -(-TILES_S // P)

BU = 7
BI = NBLK // BU
assert BU * BI == NBLK
CUTOFF = 2.0


def passed(eng, sem):
    eng.sem_inc(sem, 1)


class Steps:

    def __init__(self, eng, sem):
        self.eng, self.sem, self.base, self.n = eng, sem, 0, 0

    def add(self, ins):
        self.n += 1
        ins.then_inc(self.sem, 1)
        return self.base + self.n

    def wait(self, value=None):
        self.eng.wait_ge(self.sem, self.base + self.n if value is None else value)

    def loop(self, i, first, per):
        self.start, self.per = self.base + self.n, per
        self.base, self.n = (i - first) * per + self.start, 0

    def end(self, count):
        assert self.n == self.per, (self.n, self.per)
        self.base, self.n = self.start + self.per * count, 0


def scope(nc, ctx):
    def sb(name, shape, dt=F32):
        return ctx.enter_context(nc.sbuf_tensor(name, shape, dt))

    def ps(name, shape, dt=F32):
        return ctx.enter_context(nc.psum_tensor(name, shape, dt))

    def sem(name):
        return ctx.enter_context(nc.semaphore(name))

    return sb, ps, sem


def registers(nc, eng, row, count, most):
    _, vals = nc.values_load_multi_w_load_instructions(
        row, engines=[eng.engine], min_val=0, max_val=most,
        skip_runtime_bounds_check_because="the schedule is clipped to the arrays when it is made")
    assert len(vals) == count
    return vals


def setup_phase(nc, io, S, keep):
    with ExitStack() as ctx:
        sb, ps, sem = scope(nc, ctx)
        wb = sb("wb", [P, DK, BASES, D])
        wf = sb("wf", [P, DK, REL, D])
        loopw = sb("loopw", [P, DK, D])
        comp = sb("comp", [P, REL * BASES])
        xt = sb("xt", [P, BU, DK, P])
        NU = 7
        outs = sb("outs", [P, NU, 2, 512])
        srci = sb("srci", [P, EC], I32)
        dsti = sb("dsti", [P, EC], I32)
        typi = sb("typi", [P, EC], I32)
        wgt = sb("wgt", [P, EC])
        a3 = sb("a3", [P, EC, 3])
        dstf = sb("dstf", [P, EC])
        keys = [sb("key_d", [P, EC]), sb("key_s", [P, EC])]
        pos = [sb("pos_d", [P, EC]), sb("pos_s", [P, EC])]
        meta = sb("meta", [P, EC, META])
        spare = wb[:, :, :, :].rearrange("p k b n -> p (k b n)")
        mask = [spare[:, k * EC:(k + 1) * EC] for k in range(2)]
        runs = [spare[:, k * EC:(k + 1) * EC] for k in range(2, 4)]
        eidx = sb("eidx", [P, EC])
        posi = sb("posi", [P, EC], I32)
        blki = posi
        cut_a, cut_b, cut_m = pos[0], pos[1], keys[0]
        cnt = sb("cnt", [P, 2 * NBLK])
        tot = sb("tot", [P, 2 * NBLK])
        cum = sb("cum", [P, 2 * NBLK])
        off = sb("off", [P, 2 * NBLK])
        nti = sb("nti", [P, 2 * NBLK], I32)
        ntf = sb("ntf", [P, 2 * NBLK])
        tend = sb("tend", [P, 2 * NBLK])
        padn = sb("padn", [P, 2 * NBLK])
        zer = sb("zer", [P, NBLK])
        iota49 = sb("iota49", [P, NBLK])
        iotac = [sb("iotac_d", [P, CD]), sb("iotac_s", [P, CS])]
        tri = sb("tri", [P, P])
        ones = sb("ones", [P, P])
        ident = keep["ident"]
        half_pi = sb("half_pi", [P, 1])
        flat3 = a3[:, :, :].rearrange("p c a -> p (c a)")
        ge = flat3[:, 0:CD * NBLK].rearrange("p (c b) -> p c b", b=NBLK)
        gep = flat3[:, CD * NBLK:2 * CD * NBLK].rearrange("p (c b) -> p c b", b=NBLK)
        sblk = [sb("sblk_d", [P, CD]), sb("sblk_s", [P, CS])]
        sbl128 = [sb("sbl128_d", [P, CD]), sb("sbl128_s", [P, CS])]
        sst = [sb("sst_d", [P, CD]), sb("sst_s", [P, CS])]
        sblki = [sb("sblki_d", [P, CD], I32), sb("sblki_s", [P, CS], I32)]
        ssti = [sb("ssti_d", [P, CD], I32), sb("ssti_s", [P, CS], I32)]
        moved = sb("moved", [P, 1])
        movedi = sb("movedi", [1, 1], I32)
        pA = ps("pA", [P, 8, 512])

        small_in = sem("small_in")
        edges_in = sem("edges_in")
        xt_in = [sem(f"xt_in{j}") for j in range(BU)]
        consts = sem("consts")
        dve_steps = sem("dve_steps")
        w_ready = sem("w_ready")
        pe_loop = sem("pe_loop")
        loop_out = sem("loop_out")
        pe_chunk = sem("pe_chunk")
        chunk_out = sem("chunk_out")
        stored = [sem(f"stored{u}") for u in range(NU)]
        act_cut = sem("act_cut")
        counted = sem("counted")
        pe_counts = sem("pe_counts")
        unsorted = sem("unsorted")
        pe_unsorted = sem("pe_unsorted")
        records = sem("records")
        schedule = sem("schedule")
        rec_out = sem("rec_out")
        sched_out = sem("sched_out")
        copied = sem("copied")
        bases_in = sem("bases_in")
        cut_go = sem("cut_go")
        st_in = sem("st_in")
        st_copied = sem("st_copied")
        pool_passed = sem("a_pool_passed")
        st_out = [sem(f"st_out{q}") for q in range(3)]
        CONSTS = 12
        st_feat = sb("st_feat", [P, G50])
        st_meta = sb("st_meta", [P, META])
        st_dst = sb("st_dst", [P, 1])
        st_pos = sb("st_pos", [P, 1], I32)
        with nc.Block() as block:

            @block.sync
            def _(sp):
                sp.dma_start(comp[:, :], io["w_comp"].broadcast_to([P, REL * BASES])).then_inc(small_in, 16)
                sp.dma_start(loopw[:, :, :], io["loop_weight"].rearrange("(k p) o -> p k o", p=P)).then_inc(small_in, 16)

                def load_x(blk, j):
                    sp.dma_start(xt[:, j, :, :], io["xT"][bass.ds(blk, 1)]
                                 .rearrange("a p (k n) -> (a p) k n", k=DK)).then_inc(xt_in[j], 16)

                for j in range(BU):
                    load_x(j, j)
                sp.dma_start(a3[:, :, :], io["attr3"].rearrange("p (c a) -> p c a", a=3)).then_inc(edges_in, 16)
                sp.dma_start(srci[:, :], io["src"]).then_inc(edges_in, 16)
                sp.dma_start(dsti[:, :], io["dst"]).then_inc(edges_in, 16)
                sp.dma_start(typi[:, :], io["etype"]).then_inc(edges_in, 16)
                sp.dma_start(wgt[:, :], io["norm"]).then_inc(edges_in, 16)
                for k in range(DK):
                    sp.dma_start(wb[:, k, :, :], io["weight"][:, k * P:(k + 1) * P, :]
                                 .rearrange("b p o -> p b o")).then_inc(bases_in, 16)
                with sp.Fori(1, BI) as i:
                    for j in range(BU):
                        sp.wait_ge(pe_loop, i * BU + (j + 1 - BU))
                        load_x(i * BU + j, j)

                def store(i, h):
                    slot, j, part = h % NU, h // 4, h % 4
                    sp.wait_ge(chunk_out, i * (8 * BU) + (2 * h + 2))
                    sp.dma_start(S["table"].rearrange("(n r) d -> n (r d)", r=REL)[
                        bass.ds((i * BU + j) * P, P), part * 1024:(part + 1) * 1024],
                        outs[:, slot, :, :].rearrange("p c n -> p (c n)")).then_inc(stored[slot], 16)

                for j in range(BU):
                    sp.wait_ge(pe_loop, NBLK - BU + j + 1)
                    load_x(j, j)
                with sp.Fori(1, BI) as i:
                    for j in range(BU):
                        for part in range(4):
                            store(i - 1, 4 * j + part)
                        sp.wait_ge(pe_chunk, i * (8 * BU) + 8 * (j + 1 - BU))
                        load_x(i * BU + j, j)
                for h in range(4 * BU):
                    store(BI - 1, h)

                sp.wait_ge(records, 1)
                sp.dma_start(S["records"].rearrange("(p c) m -> p (c m)", p=P),
                             meta[:, :, :].rearrange("p c m -> p (c m)")).then_inc(rec_out, 16)
                sp.dma_start(S["dst"].rearrange("(p c) m -> p (c m)", p=P), dstf[:, :]).then_inc(rec_out, 16)
                sp.wait_ge(schedule, 2)
                for k in range(2):
                    for to, of in ((S["start"], ssti), (S["block"], sblki), (S["first_node"], sbl128)):
                        cols = of[k].shape[1]
                        sp.dma_start(to[k:k + 1, 0:cols * P].rearrange("a (p c) -> p (a c)", p=P),
                                     of[k][:, :]).then_inc(sched_out, 16)
                sp.wait_ge(sched_out, 96)
                sp.wait_ge(rec_out, 32)
                for u in range(NU):
                    sp.wait_ge(stored[u], 16 * 4 * BI)

            @block.gpsimd
            def _(pool):
                g = nc.gpsimd
                c = Steps(pool, consts)
                c.add(g.iota(iota49[:, :], [[1, NBLK]], base=0, channel_multiplier=0, allow_small_or_imprecise_dtypes=True))
                for k, cols in enumerate((CD, CS)):
                    c.add(g.iota(iotac[k][:, :], [[1, cols]], base=0, channel_multiplier=cols, allow_small_or_imprecise_dtypes=True))
                c.add(g.iota(eidx[:, :], [[1, EC]], base=0, channel_multiplier=EC, allow_small_or_imprecise_dtypes=True))
                c.add(g.iota(keep["iota_row"][:, :], [[1, P]], base=0, channel_multiplier=0, allow_small_or_imprecise_dtypes=True))
                c.add(g.memset(ident[:, :], 0.0))
                c.add(g.memset(tri[:, :], 1.0))
                c.add(g.memset(ones[:, :], 1.0))
                c.add(g.memset(zer[:, :], 0.0))
                c.add(g.memset(half_pi[:, :], math.pi / 2))
                c.wait()
                c.add(g.affine_select(out=ident[:, :], in_=ident[:, :], compare_op=ALU.not_equal, fill=1.0,
                                      base=0, pattern=[[-1, P]], channel_multiplier=1))
                c.add(g.affine_select(out=tri[:, :], in_=tri[:, :], compare_op=ALU.is_gt, fill=0.0,
                                      base=0, pattern=[[1, P]], channel_multiplier=-1))
                assert c.n == CONSTS
                pool.wait_ge(w_ready, 1)
                pool.dma_start(S["attr50"].rearrange("(a r) c -> a (r c)", r=52),
                               io["attr50"].rearrange("(a r) c -> a (r c)", r=52)).then_inc(copied, 16)
                pool.wait_ge(copied, 16)

            @block.scalar
            def _(act):
                act.wait_ge(cut_go, 1)
                nc.scalar.activation(cut_b[:, :], cut_a[:, :], ACT.Sqrt).then_inc(act_cut, 1)
                act.wait_ge(cut_go, 2)
                act.wait_ge(consts, CONSTS)
                nc.scalar.activation(cut_b[:, :], cut_a[:, :], ACT.Sin, bias=half_pi[:, :],
                                     scale=-math.pi / (2 * CUTOFF)).then_inc(act_cut, 1)
                with act.Fori(0, BI) as i:
                    for j in range(BU):
                        act.wait_ge(pe_loop, i * BU + (j + 1))
                        nc.scalar.copy(keep["acc"][:, bass.ds(i * BU + j, 1), :].rearrange("p a n -> p (a n)"),
                                       pA[:, j, 0:D]).then_inc(loop_out, 1)

                def chunks(i, first):
                    for h in range(4 * BU):
                        slot = h % NU
                        if not (first and h < NU):
                            act.wait_ge(stored[slot], i * 64 + 16 * (h // NU))
                        for q in range(2):
                            act.wait_ge(pe_chunk, i * (8 * BU) + (2 * h + q + 1))
                            nc.scalar.copy(outs[:, slot, q, :], pA[:, (2 * h + q) % 4, :]).then_inc(chunk_out, 1)

                chunks(0, True)
                with act.Fori(1, BI) as i:
                    chunks(i, False)

            @block.tensor
            def _(pe):
                pe.wait_ge(small_in, 32)

                def loop_block(i, j, first):
                    pe.wait_ge(xt_in[j], i * 16 + 16)
                    if not first:
                        pe.wait_ge(loop_out, i * BU + (j + 1 - BU))
                    for k in range(DK):
                        ins = nc.tensor.matmul(pA[:, j, 0:D], xt[:, j, k, :], loopw[:, k, :],
                                               start=(k == 0), stop=(k == DK - 1))
                    ins.then_inc(pe_loop, 1)

                for j in range(BU):
                    loop_block(0, j, True)
                with pe.Fori(1, BI) as i:
                    for j in range(BU):
                        loop_block(i, j, False)
                pe.wait_ge(w_ready, 1)
                pe.wait_ge(loop_out, NBLK)

                def table_block(i, j, first):
                    pe.wait_ge(xt_in[j], i * 16 + 16 * (BI + 1))
                    for c in range(8):
                        q = c % 4
                        if not (first and c < 4 and j == 0):
                            pe.wait_ge(chunk_out, i * (8 * BU) + (8 * j + c - 3))
                        for k in range(DK):
                            ins = nc.tensor.matmul(pA[:, q, :], xt[:, j, k, :],
                                                   wf[:, k, 2 * c:2 * c + 2, :].rearrange("p r n -> p (r n)"),
                                                   start=(k == 0), stop=(k == DK - 1))
                        ins.then_inc(pe_chunk, 1)

                for i in range(2):
                    for j in range(BU):
                        table_block(i, j, i == 0)
                pe.wait_ge(consts, CONSTS)
                pe.wait_ge(counted, 1)
                nc.tensor.matmul(pA[:, 5, 0:2 * NBLK], ones[:, :], cnt[:, :], start=True, stop=True)
                nc.tensor.matmul(pA[:, 6, 0:2 * NBLK], tri[:, :], cnt[:, :], start=True, stop=True).then_inc(pe_counts, 1)
                with pe.Fori(2, BI) as i:
                    for j in range(BU):
                        table_block(i, j, False)
                pe.wait_ge(unsorted, 1)
                nc.tensor.matmul(pA[0:1, 7, 0:1], moved[:, :], ones[:, 0:1], start=True, stop=True).then_inc(pe_unsorted, 1)

            @block.vector
            def _(v):
                vv = nc.vector
                s = Steps(v, dve_steps)
                v.wait_ge(edges_in, 80)
                s.add(vv.tensor_tensor(a3[:, :, :], a3[:, :, :], a3[:, :, :], ALU.mult))
                s.wait()
                s.add(vv.tensor_tensor(cut_a[:, :], a3[:, :, 0], a3[:, :, 1], ALU.add))
                s.wait()
                vv.tensor_tensor(cut_a[:, :], cut_a[:, :], a3[:, :, 2], ALU.add).then_inc(cut_go, 1)
                s.add(vv.scalar_tensor_tensor(meta[:, :, M_ROW].bitcast(I32), srci[:, :], float(REL), typi[:, :],
                                              ALU.mult, ALU.add))
                s.wait()
                s.add(vv.tensor_scalar(meta[:, :, M_ROW].bitcast(I32), meta[:, :, M_ROW].bitcast(I32),
                                       float(NBLK * P * REL - 1), None, ALU.min))
                s.add(vv.tensor_copy(meta[:, :, M_NORM], wgt[:, :]))
                s.add(vv.tensor_copy(dstf[:, :], dsti[:, :]))
                s.add(vv.tensor_copy(meta[:, :, M_DST], dsti[:, :]))
                s.add(vv.tensor_copy(meta[:, :, M_SRC], srci[:, :]))
                v.wait_ge(act_cut, 1)
                s.add(vv.tensor_scalar(cut_m[:, :], cut_b[:, :], CUTOFF, None, ALU.is_le))
                vv.tensor_scalar(cut_a[:, :], cut_b[:, :], CUTOFF, None, ALU.min).then_inc(cut_go, 1)
                v.wait_ge(small_in, 32)
                v.wait_ge(bases_in, 16 * DK)
                for r in range(REL):
                    s.add(vv.tensor_scalar(wf[:, :, r, :], wb[:, :, 0, :], comp[:, r * BASES:r * BASES + 1], None, ALU.mult))
                with v.Fori(1, BASES) as b:
                    s.loop(b, 1, REL)
                    for r in range(REL):
                        s.wait(s.base + r + 1 - REL)
                        s.add(vv.scalar_tensor_tensor(
                            wf[:, :, r, :], wb[:, :, bass.ds(b, 1), :].rearrange("p k a n -> p k (a n)"),
                            comp[:, bass.ds(b + r * BASES, 1)], wf[:, :, r, :], ALU.mult, ALU.add))
                s.end(BASES - 1)
                s.wait()
                vv.memset(moved[:, :], 0.0).then_inc(w_ready, 1)
                v.wait_ge(act_cut, 2)
                s.add(vv.tensor_tensor(cut_b[:, :], cut_b[:, :], cut_b[:, :], ALU.mult))
                s.wait()
                s.add(vv.tensor_tensor(meta[:, :, M_CUT], cut_b[:, :], cut_m[:, :], ALU.mult))
                v.wait_ge(consts, CONSTS)
                for k, of in enumerate((dsti, srci)):
                    s.wait()
                    s.add(vv.tensor_scalar(blki[:, :], of[:, :], 7, None, ALU.arith_shift_right))
                    s.wait()
                    s.add(vv.tensor_copy(keys[k][:, :], blki[:, :]))
                    s.wait()
                    s.add(vv.scalar_tensor_tensor(pos[k][:, :], keys[k][:, :], float(NBLK), eidx[:, :], ALU.is_equal, ALU.mult))
                with v.Fori(0, NBLK) as b:
                    s.loop(b, 0, 2)
                    for k in range(2):
                        s.wait(s.base + s.n - 1)
                        s.add(vv.tensor_scalar(mask[k], keys[k][:, :], iota49[:, bass.ds(b, 1)], None,
                                               ALU.is_equal, ALU.add, accum_out=cnt[:, bass.ds(b + k * NBLK, 1)]))
                s.end(NBLK)
                s.wait()
                vv.memset(moved[:, :], 0.0).then_inc(counted, 1)
                v.wait_ge(pe_counts, 1)
                s.add(vv.tensor_copy(tot[:, :], pA[:, 5, 0:2 * NBLK]))
                s.wait()
                for k in range(2):
                    h = slice(k * NBLK, (k + 1) * NBLK)
                    s.add(vv.tensor_tensor_scan(cum[:, h], tot[:, h], zer[:, :], 0.0, ALU.add, ALU.add))
                s.wait()
                s.add(vv.tensor_tensor(off[:, :], cum[:, :], tot[:, :], ALU.subtract))
                s.wait()
                s.add(vv.scalar_tensor_tensor(off[:, :], off[:, :], -1.0, pA[:, 6, 0:2 * NBLK], ALU.add, ALU.add))
                with v.Fori(0, NBLK) as b:
                    s.loop(b, 0, 8)
                    s.wait()
                    for k in range(2):
                        s.add(vv.tensor_scalar(mask[k], keys[k][:, :], iota49[:, bass.ds(b, 1)], None, ALU.is_equal))
                    for k in range(2):
                        s.wait(s.base + 1 + k)
                        s.add(vv.tensor_tensor_scan(runs[k], mask[k], mask[k],
                                                    off[:, bass.ds(b + k * NBLK, 1)], ALU.add, ALU.bypass))
                    for k in range(2):
                        s.wait(s.base + 3 + k)
                        s.add(vv.tensor_tensor(runs[k], runs[k], mask[k], ALU.mult))
                    for k in range(2):
                        s.wait(s.base + 5 + k)
                        s.add(vv.tensor_tensor(pos[k][:, :], pos[k][:, :], runs[k], ALU.add))
                s.end(NBLK)
                s.wait()
                vv.tensor_copy(meta[:, :, M_SLOT], pos[1][:, :]).then_inc(records, 1)
                s.add(vv.tensor_copy(posi[:, :], pos[0][:, :]))
                s.add(vv.tensor_tensor(mask[0], pos[0][:, :], eidx[:, :], ALU.not_equal))
                s.wait()
                vv.reduce_sum(moved[:, :], mask[0], AXX).then_inc(unsorted, 1)
                for k, (size, cols) in enumerate(((P, CD), (PAIR, CS))):
                    h = slice(k * NBLK, (k + 1) * NBLK)
                    s.add(vv.tensor_scalar(nti[:, h], tot[:, h], float(size - 1), None, ALU.add))
                    s.wait()
                    s.add(vv.tensor_scalar(nti[:, h], nti[:, h], size.bit_length() - 1, None, ALU.arith_shift_right))
                    s.wait()
                    s.add(vv.tensor_copy(ntf[:, h], nti[:, h]))
                    s.wait()
                    s.add(vv.tensor_tensor_scan(tend[:, h], ntf[:, h], zer[:, :], 0.0, ALU.add, ALU.add))
                    s.add(vv.scalar_tensor_tensor(padn[:, h], ntf[:, h], float(size), tot[:, h], ALU.mult, ALU.subtract))
                    s.wait()
                    both = [P, cols, NBLK]
                    s.add(vv.tensor_tensor(ge[:, 0:cols, :], iotac[k][:, :].rearrange("p (c a) -> p c a", a=1).broadcast_to(both),
                                           tend[:, h].rearrange("p (a b) -> p a b", a=1).broadcast_to(both), ALU.is_ge))
                    s.wait()
                    s.add(vv.tensor_tensor(gep[:, 0:cols, :], ge[:, 0:cols, :],
                                           padn[:, h].rearrange("p (a b) -> p a b", a=1).broadcast_to(both), ALU.mult))
                    s.add(vv.reduce_sum(sblk[k][:, :], ge[:, 0:cols, :], AXX))
                    s.wait()
                    s.add(vv.reduce_sum(sst[k][:, :], gep[:, 0:cols, :], AXX))
                    s.add(vv.tensor_scalar(sblk[k][:, :], sblk[k][:, :], float(NBLK - 1), None, ALU.min))
                    s.wait()
                    s.add(vv.scalar_tensor_tensor(sst[k][:, :], iotac[k][:, :], float(size), sst[k][:, :], ALU.mult, ALU.subtract))
                    s.add(vv.tensor_scalar(sbl128[k][:, :], sblk[k][:, :], float(P), None, ALU.mult))
                    s.add(vv.tensor_copy(sblki[k][:, :], sblk[k][:, :]))
                    s.wait()
                    vv.tensor_scalar(ssti[k][:, :], sst[k][:, :], float(E), None, ALU.min).then_inc(schedule, 1)
                v.wait_ge(pe_unsorted, 1)
                s.add(vv.tensor_copy(movedi[:, :], pA[0:1, 7, 0:1]))

        with nc.Block() as block_sort:

            @block_sort.gpsimd
            def _(pool):
                g = nc.gpsimd
                (flag,) = registers(nc, pool, movedi[0:1, 0:1], 1, EP)
                with pool.If(flag > 0):
                    with pool.Fori(0, EC) as c:
                        pool.dma_start(st_feat[:, :], io["attr50"].rearrange("(p c) m -> p (c m)", p=P)[
                            :, bass.ds(c * G50, G50)]).then_inc(st_in, 16)
                        g.tensor_copy(st_meta[:, :], meta[:, bass.ds(c, 1), :].rearrange("p a m -> p (a m)")).then_inc(st_copied, 1)
                        g.tensor_copy(st_dst[:, :], dstf[:, bass.ds(c, 1)]).then_inc(st_copied, 1)
                        g.tensor_copy(st_pos[:, :], posi[:, bass.ds(c, 1)]).then_inc(st_copied, 1)
                        pool.wait_ge(st_copied, c * 3 + 3)
                        pool.wait_ge(st_in, c * 16 + 16)
                        passed(pool, pool_passed)
                        for q, (to, of) in enumerate((("attr50", st_feat), ("records", st_meta), ("dst", st_dst))):
                            g.indirect_dma_start(out=S[to], out_offset=bass.IndirectOffsetOnAxis(ap=st_pos[:, 0:1], axis=0),
                                                 in_=of[:, :], in_offset=None).then_inc(st_out[q], 16)
                        for q in range(3):
                            pool.wait_ge(st_out[q], c * 16 + 16)
                        passed(pool, pool_passed)
                with pool.Else():
                    g.memset(st_dst[:, :], 0.0)


def load_schedule(sp, S, k, cols, start, block, first, ready):
    sp.dma_start(start[:, :], S["start"][k:k + 1, 0:cols * P]).then_inc(ready, 16)
    sp.dma_start(block[:, :], S["block"][k:k + 1, 0:cols * P]).then_inc(ready, 16)
    sp.dma_start(first[:, :], S["first_node"][k:k + 1, 0:cols * P].broadcast_to([P, cols * P])).then_inc(ready, 16)


def relation_phase(nc, io, S, keep):
    U, H = B_UNROLL, B_UNROLL // 2
    ITER = TILES_D // U
    NPS = 4
    acc = keep["acc"]
    with ExitStack() as ctx:
        sb, ps, sem = scope(nc, ctx)
        start = sb("b_start", [1, CD * P], I32)
        blk = sb("b_blk", [1, CD * P], I32)
        first = sb("b_first", [P, CD * P])
        meta = sb("b_meta", [P, U, META])
        rows = sb("b_rows", [P, U, D])
        local = sb("b_local", [P, U])
        mask = sb("b_mask", [P, U, P])
        pB = ps("pB", [P, NPS, 512])
        sched = sem("b_sched")
        meta_in = [sem(f"b_meta_in{h}") for h in range(2)]
        rows_in = [sem(f"b_rows_in{u}") for u in range(U)]
        local_done = sem("b_local_done")
        mask_done = sem("b_mask_done")
        pool_passed = sem("b_pool_passed")
        mult = sem("b_mult")
        added = sem("b_added")

        with nc.Block() as block:
            @block.sync
            def _(sp):
                load_schedule(sp, S, 0, CD, start, blk, first, sched)
                sp.wait_ge(sched, 48)

                def half(i, h, peeled):
                    at = registers(nc, sp, start[0:1, bass.ds(i * U + h * H, H)], H, E)
                    for u in range(H):
                        if not peeled:
                            sp.wait_ge(mult, i * U + (h * H + u + 1 - U))
                        sp.dma_start(meta[:, h * H + u, :], S["records"][bass.ds(at[u], P), :]).then_inc(meta_in[h], 16)

                for h in range(2):
                    half(0, h, True)
                with sp.Fori(1, ITER) as i:
                    for h in range(2):
                        half(i, h, False)

            @block.gpsimd
            def _(pool):
                def half(i, h, peeled):
                    pool.wait_ge(meta_in[h], i * (16 * H) + 16 * H)
                    for u in range(h * H, h * H + H):
                        if not peeled:
                            pool.wait_ge(mult, i * U + (u + 1 - U))
                        passed(pool, pool_passed)
                        nc.gpsimd.indirect_dma_start(
                            out=rows[:, u, :], out_offset=None, in_=S["table"],
                            in_offset=bass.IndirectOffsetOnAxis(ap=meta[:, u, M_ROW:M_ROW + 1].bitcast(I32), axis=0),
                        ).then_inc(rows_in[u], 16)

                for h in range(2):
                    half(0, h, True)
                with pool.Fori(1, ITER) as i:
                    for h in range(2):
                        half(i, h, False)

            @block.tensor
            def _(pe):
                def tile(i, u, peeled):
                    if not (peeled and u < NPS):
                        pe.wait_ge(added, i * U + (u + 1 - NPS))
                    pe.wait_ge(mask_done, i * U + (u + 1))
                    pe.wait_ge(rows_in[u], i * 16 + 16)
                    nc.tensor.matmul(pB[:, u % NPS, 0:D], mask[:, u, :], rows[:, u, :],
                                     start=True, stop=True).then_inc(mult, 1)

                for u in range(U):
                    tile(0, u, True)
                with pe.Fori(1, ITER) as i:
                    for u in range(U):
                        tile(i, u, False)

            @block.vector
            def _(v):
                vv = nc.vector

                def masks(i, h, peeled):
                    v.wait_ge(meta_in[h], i * (16 * H) + 16 * H)
                    if not peeled:
                        v.wait_ge(mult, i * U + (h * H + H - U))
                    u0 = h * H
                    vv.tensor_tensor(local[:, u0:u0 + H], meta[:, u0:u0 + H, M_DST],
                                     first[:, bass.ds(i * U + u0, H)], ALU.subtract).then_inc(local_done, 1)
                    v.wait_ge(local_done, i * 2 + (h + 1))
                    for u in range(u0, u0 + H):
                        vv.tensor_scalar(mask[:, u, :], keep["iota_row"][:, :], local[:, u:u + 1],
                                         meta[:, u, M_NORM:M_NORM + 1], ALU.is_equal, ALU.mult).then_inc(mask_done, 1)

                def adds(i, h, peeled):
                    at = registers(nc, v, blk[0:1, bass.ds(i * U + h * H, H)], H, NBLK - 1)
                    for u in range(H):
                        t = h * H + u
                        v.wait_ge(mult, i * U + (t + 1))
                        if not (peeled and t == 0):
                            v.wait_ge(added, i * U + t)
                        to = acc[:, bass.ds(at[u], 1), :].rearrange("p a n -> p (a n)")
                        vv.tensor_tensor(to, pB[:, t % NPS, 0:D], to, ALU.add).then_inc(added, 1)

                v.wait_ge(sched, 48)
                masks(0, 0, True)
                masks(0, 1, True)
                adds(0, 0, True)
                with v.Fori(1, ITER) as i:
                    masks(i, 0, False)
                    adds(i - 1, 1, False)
                    masks(i, 1, False)
                    adds(i, 0, False)
                adds(ITER - 1, 1, False)


def norm_phase(nc, io, S, keep):
    acc = keep["acc"]
    y3 = keep["y3"]
    with ExitStack() as ctx:
        sb, ps, sem = scope(nc, ctx)
        bias = sb("t_bias", [P, D])
        lin1 = sb("t_lin1", [P, DK, D])
        xin = sb("t_x", [P, BU, D])
        h = sb("t_h", [P, BU, D])
        stats = sb("t_stats", [P, BU, 6])
        mv = sb("t_mv", [P, BU, 2])
        eps = sb("t_eps", [P, 1])
        std = sb("t_std", [P, BU])
        rstd = sb("t_rstd", [P, BU])
        x1 = sb("t_x1", [P, BU, D])
        x1T = sb("t_x1T", [P, BU, DK, P])
        rest = sb("t_rest", [P, BU, D])
        pX = ps("pX", [P, 3, 512])
        pY = ps("pY", [P, 2, 512])
        const_in = sem("t_const_in")
        x_in = [sem(f"t_x_in{j}") for j in range(BU)]
        v_passed = sem("t_v_passed")
        dve = sem("t_dve")
        std_go = sem("t_std_go")
        std_done = sem("t_std_done")
        x1_done = sem("t_x1_done")
        x1_kept = sem("t_x1_kept")
        turned = sem("t_turned")
        x1T_done = sem("t_x1T_done")
        y_done = sem("t_y_done")
        y_hi = sem("t_y_hi")
        y_all = sem("t_y_all")

        def at(a, b, *mid):
            return a[(slice(None), bass.ds(b, 1)) + mid]

        with nc.Block() as block:
            @block.sync
            def _(sp):
                sp.dma_start(bias[:, :], io["h_bias"].broadcast_to([P, D])).then_inc(const_in, 16)
                sp.dma_start(lin1[:, :, :], io["lin1"].rearrange("(k p) o -> p k o", p=P)).then_inc(const_in, 16)
                for j in range(BU):
                    sp.dma_start(xin[:, j, :], io["x"][j * P:(j + 1) * P, :]).then_inc(x_in[j], 16)
                with sp.Fori(1, BI) as i:
                    for j in range(BU):
                        sp.wait_ge(x1_done, i * BU + (j + 1 - BU))
                        sp.dma_start(xin[:, j, :], io["x"][bass.ds((i * BU + j) * P, P), :]).then_inc(x_in[j], 16)

            @block.gpsimd
            def _(pool):
                with pool.Fori(0, BI) as i:
                    for j in range(BU):
                        pool.wait_ge(x1_done, i * BU + (j + 1))
                        nc.gpsimd.tensor_copy(at(acc, i * BU + j).rearrange("p a n -> p (a n)"), x1[:, j, :]).then_inc(x1_kept, 1)

            @block.vector
            def _(v):
                vv = nc.vector
                s = Steps(v, dve)
                s.add(vv.memset(eps[:, :], 1e-5))
                v.wait_ge(const_in, 32)

                def parts(i, j):
                    v.wait_ge(y_hi, i * BU + (j + 1))
                    b = i * BU + j
                    hi, mid, lo = (y3[:, bass.ds(b, 1), q, :].rearrange("p a n -> p (a n)") for q in range(3))
                    s.add(vv.tensor_tensor(rest[:, j, :], pY[:, j % 2, 0:D], hi, ALU.subtract))
                    s.wait()
                    s.add(vv.tensor_copy(mid, rest[:, j, :]))
                    s.wait()
                    vv.tensor_tensor(lo, rest[:, j, :], mid, ALU.subtract).then_inc(y_all, 1)

                def norm(i, j):
                    v.wait_ge(x_in[j], i * 16 + 16)
                    s.add(vv.tensor_tensor(h[:, j, :], at(acc, i * BU + j).rearrange("p a n -> p (a n)"), bias[:, :], ALU.add))
                    s.wait()
                    s.add(vv.scalar_tensor_tensor(h[:, j, :], h[:, j, :], 0.0, xin[:, j, :], ALU.max, ALU.add))
                    s.wait()
                    passed(v, v_passed)
                    s.add(vv.bn_stats(stats[:, j, :], h[:, j, :]))
                    s.wait()
                    passed(v, v_passed)
                    vv.bn_aggr(mv[:, j, :], stats[:, j, :]).then_inc(std_go, 1)

                def apply(i, j, peeled):
                    v.wait_ge(std_done, i * BU + (j + 1))
                    s.add(vv.reciprocal(rstd[:, j:j + 1], std[:, j:j + 1]))
                    s.wait()
                    if not peeled:
                        v.wait_ge(x1_kept, i * BU + (j + 1 - BU))
                        v.wait_ge(turned, i * BU + (j + 1 - BU))
                    vv.tensor_scalar(x1[:, j, :], h[:, j, :], mv[:, j, 0:1], rstd[:, j:j + 1],
                                     ALU.subtract, ALU.mult).then_inc(x1_done, 1)

                norm(0, 0)
                for j in range(BU):
                    if j + 1 < BU:
                        norm(0, j + 1)
                    apply(0, j, True)
                    if j >= 2:
                        parts(0, j - 2)
                with v.Fori(1, BI) as i:
                    s.loop(i, 1, 6 * BU)
                    for j in range(BU):
                        if j == 0:
                            norm(i, 0)
                        if j + 1 < BU:
                            norm(i, j + 1)
                        apply(i, j, False)
                        parts(i - 1 if j < 2 else i, (j - 2) % BU)
                s.end(BI - 1)
                parts(BI - 1, BU - 2)
                parts(BI - 1, BU - 1)

            @block.scalar
            def _(act):
                def root(i, j):
                    act.wait_ge(std_go, i * BU + (j + 1))
                    nc.scalar.activation(std[:, j:j + 1], mv[:, j, 1:2], ACT.Sqrt, bias=eps[:, :]).then_inc(std_done, 1)

                def keep_turned(i, j, peeled):
                    act.wait_ge(turned, i * BU + (j + 1))
                    if not peeled:
                        act.wait_ge(y_done, i * BU + (j + 1 - BU))
                    nc.scalar.copy(x1T[:, j, :, :].rearrange("p k n -> p (k n)"), pX[:, j % 3, 0:D]).then_inc(x1T_done, 1)

                def high(i, j):
                    act.wait_ge(y_done, i * BU + (j + 1))
                    nc.scalar.copy(y3[:, bass.ds(i * BU + j, 1), 0, :].rearrange("p a n -> p (a n)"),
                                   pY[:, j % 2, 0:D]).then_inc(y_hi, 1)

                def body(i, peeled):
                    for j in range(BU):
                        if j == 0:
                            root(i, 0)
                        if j + 1 < BU:
                            root(i, j + 1)
                        keep_turned(i, j, peeled)
                        if not (peeled and j == 0):
                            high(i - 1 if j == 0 else i, (j - 1) % BU)

                act.wait_ge(dve, 1)
                body(0, True)
                with act.Fori(1, BI) as i:
                    body(i, False)
                high(BI - 1, BU - 1)

            @block.tensor
            def _(pe):
                def turn(i, j, peeled):
                    pe.wait_ge(x1_done, i * BU + (j + 1))
                    if not (peeled and j < 3):
                        pe.wait_ge(x1T_done, i * BU + (j - 1 if j else 0))
                    for k in range(DK):
                        ins = nc.tensor.transpose(pX[:, j % 3, k * P:(k + 1) * P], x1[:, j, k * P:(k + 1) * P], keep["ident"][:, :])
                    ins.then_inc(turned, 1)

                def multiply(i, j, peeled):
                    pe.wait_ge(x1T_done, i * BU + (j + 1))
                    if not (peeled and j < 2):
                        pe.wait_ge(y_all, i * BU + (j - 1 if j else 0))
                    for k in range(DK):
                        ins = nc.tensor.matmul(pY[:, j % 2, 0:D], x1T[:, j, k, :], lin1[:, k, :],
                                               start=(k == 0), stop=(k == DK - 1))
                    ins.then_inc(y_done, 1)

                def body(i, peeled):
                    for j in range(BU):
                        turn(i, j, peeled)
                        if not (peeled and j == 0):
                            multiply(i - 1 if j == 0 else i, (j - 1) % BU, peeled)

                pe.wait_ge(const_in, 32)
                body(0, True)
                with pe.Fori(1, BI) as i:
                    body(i, False)
                multiply(BI - 1, BU - 1, False)


def edge_phase(nc, io, S, keep):
    T = 4
    G = TILES_D // T
    KA = G50 + 1
    HALF = P // 2
    y3, ident = keep["y3"], keep["ident"]
    with ExitStack() as ctx:
        sb, ps, sem = scope(nc, ctx)
        start = sb("c_start", [1, CD * P], I32)
        blk = sb("c_blk", [1, CD * P], I32)
        first = sb("c_first", [P, CD * P])
        w1 = sb("c_w1", [P, P])
        w2 = sb("c_w2", [P, DK, D])
        b2 = sb("c_b2", [P, D])
        ident_b = sb("c_ident_b", [P, P], BF16)
        half_one = sb("c_half_one", [P, 1])
        feat = sb("c_feat", [P, 2 * T, 2, HALF])
        meta = sb("c_meta", [P, 2 * T, META])
        ends = sb("c_ends", [P, 2 * T, P], BF16)
        pick = sb("c_pick", [P, 2, T * P], BF16)
        local = sb("c_local", [P, 2, T])
        late = sb("c_late", [P, 2, T])
        slot = sb("c_slot", [P, 2, T], I32)
        featT = sb("c_featT", [P, 2, T * P])
        soft = sb("c_soft", [P, 2, DK, T * P])
        hid = sb("c_hid", [P, 2, DK, T * P])
        wgt = sb("c_wgt", [P, T, D])
        msg = sb("c_msg", [P, 2 * T, MSG])
        pT = ps("pT", [P, 512])
        pP = ps("pP", [P, 1024], BF16)
        pH = ps("pH", [P, 2, DK, 512])
        pW = ps("pW", [P, 2, 512])

        sched = sem("c_sched")
        pool_passed = sem("c_pool_passed")
        pe_passed = sem("c_pe_passed")
        const_in = sem("c_const_in")
        consts = sem("c_consts")
        fill_out = sem("c_fill_out")
        feat_in = [sem(f"c_feat_in{q}") for q in range(2)]
        meta_in = [sem(f"c_meta_in{q}") for q in range(2)]
        turned = sem("c_turned")
        featT_done = sem("c_featT_done")
        layer1 = sem("c_layer1")
        soft_step = sem("c_soft_step")
        hid_done = sem("c_hid_done")
        ends_done = sem("c_ends_done")
        ends_turned = sem("c_ends_turned")
        pick_done = sem("c_pick_done")
        tile_done = sem("c_tile_done")
        biased = sem("c_biased")
        local_done = sem("c_local_done")
        small = sem("c_small")
        msg_done = sem("c_msg_done")
        sent = [sem(f"c_sent{u}") for u in range(2 * T)]

        with nc.Block() as block:
            @block.sync
            def _(sp):
                load_schedule(sp, S, 0, CD, start, blk, first, sched)
                for k in range(DK):
                    sp.dma_start(w1[k * HALF:k * HALF + G50, :], io["w1"][:, k * P:(k + 1) * P]).then_inc(const_in, 16)
                    sp.dma_start(w1[k * HALF + G50:k * HALF + KA, :], io["b1"][:, k * P:(k + 1) * P]).then_inc(const_in, 16)
                sp.dma_start(w2[:, :, :], io["w2"].rearrange("(k p) o -> p k o", p=P)).then_inc(const_in, 16)
                sp.dma_start(b2[:, :], io["b2"].broadcast_to([P, D])).then_inc(const_in, 16)
                sp.wait_ge(consts, 4)
                sp.dma_start(S["messages"][E:E + PAIR, :].rearrange("(p j) m -> p (j m)", j=2),
                             msg[:, 0:2, :].rearrange("p j m -> p (j m)")).then_inc(fill_out, 16)
                sp.wait_ge(sched, 48)

                def feats(g, q):
                    at = registers(nc, sp, start[0:1, bass.ds(g * T, T)], T, E)
                    for t in range(T):
                        sp.dma_start(feat[:, q * T + t, :, 0:G50],
                                     S["attr50"][bass.ds(at[t], P), :].rearrange("e (a c) -> e a c", a=1)
                                     .broadcast_to([P, 2, G50])).then_inc(feat_in[q], 16)

                def metas(g, q):
                    at = registers(nc, sp, start[0:1, bass.ds(g * T, T)], T, E)
                    for t in range(T):
                        sp.dma_start(meta[:, q * T + t, :], S["records"][bass.ds(at[t], P), :]).then_inc(meta_in[q], 16)

                def turn(i, q, feats_ahead, metas_ahead, peeled):
                    g = i * 2 + q
                    if metas_ahead:
                        if not (peeled and q == 0):
                            sp.wait_ge(msg_done, g * T)
                        metas(g + 1, 1 - q)
                    if feats_ahead:
                        sp.wait_ge(turned, g + 2)
                        feats(g + 3, 1 - q)

                feats(0, 0)
                feats(1, 1)
                metas(0, 0)
                sp.wait_ge(turned, 1)
                feats(2, 0)
                for q in range(2):
                    turn(0, q, True, True, True)
                with sp.Fori(1, G // 2 - 2) as i:
                    for q in range(2):
                        turn(i, q, True, True, False)
                for g in range(G - 4, G):
                    turn(g // 2, g % 2, g + 3 < G, g + 1 < G, False)
                sp.wait_ge(fill_out, 16)

            @block.gpsimd
            def _(pool):
                g_ = nc.gpsimd
                g_.memset(msg[:, :, :], 0.0).then_inc(consts, 1)
                g_.tensor_copy(ident_b[:, :], ident[:, :]).then_inc(consts, 1)
                g_.memset(half_one[:, :], 0.5).then_inc(consts, 1)
                pool.wait_ge(consts, 3)
                g_.memset(msg[:, 0:2, D], float(PADNODE)).then_inc(consts, 1)
                g_.memset(feat[:, :, :, G50:HALF], 1.0).then_inc(consts, 1)

                def tile(i, u):
                    pool.wait_ge(msg_done, i * (2 * T) + (u + 1))
                    passed(pool, pool_passed)
                    g_.indirect_dma_start(
                        out=S["messages"], out_offset=bass.IndirectOffsetOnAxis(ap=slot[:, u // T, u % T:u % T + 1], axis=0),
                        in_=msg[:, u, :], in_offset=None, bounds_check=E - 1, oob_is_err=False).then_inc(sent[u], 16)

                with pool.Fori(0, G // 2) as i:
                    for u in range(2 * T):
                        tile(i, u)
                for u in range(2 * T):
                    pool.wait_ge(sent[u], 16 * (G // 2))

            @block.tensor
            def _(pe):
                def turn_features(g, i, q, peeled):
                    pe.wait_ge(feat_in[q], i * (16 * T) + 16 * T)
                    if not peeled:
                        pe.wait_ge(featT_done, g)
                    passed(pe, pe_passed)
                    for t in range(T):
                        ins = nc.tensor.transpose(pT[:, t * P:(t + 1) * P],
                                                  feat[:, q * T + t, :, :].rearrange("p a c -> p (a c)"), ident[:, :])
                    ins.then_inc(turned, 1)

                def turn_ends(g, q, peeled):
                    pe.wait_ge(ends_done, g + 1)
                    if not peeled:
                        pe.wait_ge(pick_done, g)
                    passed(pe, pe_passed)
                    for t in range(T):
                        ins = nc.tensor.transpose(pP[:, t * P:(t + 1) * P], ends[:, q * T + t, :], ident_b[:, :])
                    ins.then_inc(ends_turned, 1)

                def first_layer(g, q, peeled):
                    pe.wait_ge(featT_done, g + 1)
                    if not peeled:
                        pe.wait_ge(hid_done, g - 1)
                    for k in range(DK):
                        rows = slice(k * HALF, k * HALF + KA)
                        ins = nc.tensor.matmul(pH[:, q, k, :], w1[rows, :], featT[rows, q, :], start=True, stop=True)
                    ins.then_inc(layer1, 1)

                def tiles(i, q, ahead1, peeled):
                    at = registers(nc, pe, blk[0:1, bass.ds(i * (2 * T) + q * T, T)], T, NBLK - 1)
                    for t in range(T):
                        u = q * T + t
                        n = i * (2 * T) + u
                        if not (peeled and u < 2):
                            pe.wait_ge(msg_done, n - 1)
                        if t == 0:
                            pe.wait_ge(pick_done, i * 2 + (q + 1))
                        for part in range(3):
                            nc.tensor.matmul(pW[:, u % 2, D:2 * D], pick[:, q, t * P:(t + 1) * P],
                                             y3[:, bass.ds(at[t], 1), part, :].rearrange("p a n -> p (a n)"),
                                             start=(part == 0), stop=(part == 2))
                        if t == 0:
                            pe.wait_ge(hid_done, i * 2 + (q + 1))
                        for k in range(DK):
                            ins = nc.tensor.matmul(pW[:, u % 2, 0:D], hid[:, q, k, t * P:(t + 1) * P], w2[:, k, :],
                                                   start=(k == 0), stop=(k == DK - 1))
                        ins.then_inc(tile_done, 1)
                        if ahead1 and t == 2:
                            turn_ends(i * 2 + (q + 1), 1 - q, False)

                def turn(i, q, ahead1, ahead2, peeled):
                    g = i * 2 + q
                    if ahead1:
                        first_layer(g + 1, 1 - q, peeled and q == 0)
                    if ahead2:
                        turn_features(g + 2, i + 1, q, False)
                    tiles(i, q, ahead1, peeled)

                pe.wait_ge(const_in, 96)
                pe.wait_ge(consts, 5)
                turn_features(0, 0, 0, True)
                first_layer(0, 0, True)
                turn_features(1, 0, 1, False)
                turn_ends(0, 0, True)
                for q in range(2):
                    turn(0, q, True, True, True)
                with pe.Fori(1, G // 2 - 1) as i:
                    for q in range(2):
                        turn(i, q, True, True, False)
                for q in range(2):
                    turn(G // 2 - 1, q, q == 0, False, False)

            @block.scalar
            def _(act):
                def soft_plus(i, q, g, step, peeled):
                    u = soft[:, q, :, :].rearrange("p k n -> p (k n)")
                    if step == 0:
                        act.wait_ge(layer1, g + 1)
                        if not peeled:
                            act.wait_ge(hid_done, g - 1)
                        nc.scalar.activation(u, pH[:, q, :, :].rearrange("p k n -> p (k n)"), ACT.Abs).then_inc(soft_step, 1)
                    elif step == 1:
                        act.wait_ge(soft_step, g * 3 + 1)
                        nc.scalar.activation(u, u, ACT.Exp, scale=-1.0).then_inc(soft_step, 1)
                    else:
                        act.wait_ge(soft_step, g * 3 + 2)
                        nc.scalar.activation(u, u, ACT.Ln, scale=0.5, bias=half_one[:, :]).then_inc(soft_step, 1)

                def keep_features(g, q, peeled):
                    act.wait_ge(turned, g + 1)
                    if not peeled:
                        act.wait_ge(layer1, g - 1)
                    nc.scalar.copy(featT[:, q, :], pT[:, :]).then_inc(featT_done, 1)

                def keep_picks(g, q, peeled):
                    act.wait_ge(ends_turned, g + 1)
                    if not peeled:
                        act.wait_ge(tile_done, (g - 1) * T)
                    nc.scalar.copy(pick[:, q, :], pP[:, 0:T * P]).then_inc(pick_done, 1)

                def turn(i, q, ahead1, ahead2, peeled):
                    g = i * 2 + q
                    if ahead1:
                        for step in range(2):
                            soft_plus(None, 1 - q, g + 1, step, peeled and q == 0)
                    if ahead2:
                        keep_features(g + 2, q, False)
                    if ahead1:
                        soft_plus(None, 1 - q, g + 1, 2, peeled and q == 0)
                        keep_picks(g + 1, 1 - q, peeled and q == 0)

                nc.scalar.preload_act_table_set("natural_log_exp_and_others")
                act.wait_ge(consts, 3)
                keep_features(0, 0, True)
                for step in range(3):
                    soft_plus(0, 0, 0, step, True)
                keep_features(1, 1, True)
                keep_picks(0, 0, True)
                for q in range(2):
                    turn(0, q, True, True, True)
                with act.Fori(1, G // 2 - 1) as i:
                    for q in range(2):
                        turn(i, q, True, True, False)
                for q in range(2):
                    turn(G // 2 - 1, q, q == 0, False, False)

            @block.vector
            def _(v):
                vv = nc.vector

                def hidden(g, q):
                    v.wait_ge(soft_step, g * 3 + 3)
                    vv.scalar_tensor_tensor(hid[:, q, :, :].rearrange("p k n -> p (k n)"),
                                            pH[:, q, :, :].rearrange("p k n -> p (k n)"), 0.0,
                                            soft[:, q, :, :].rearrange("p k n -> p (k n)"), ALU.max, ALU.add).then_inc(hid_done, 1)

                def find_ends(i, q, peeled):
                    g = i * 2 + q
                    m = slice(q * T, q * T + T)
                    v.wait_ge(meta_in[q], i * (16 * T) + 16 * T)
                    vv.tensor_tensor(local[:, q, :], meta[:, m, M_DST], first[:, bass.ds(g * T, T)], ALU.subtract).then_inc(local_done, 1)
                    v.wait_ge(local_done, g + 1)
                    if not peeled:
                        v.wait_ge(ends_turned, g - 1)
                    for t in range(T):
                        ins = vv.tensor_scalar(ends[:, q * T + t, :], keep["iota_row"][:, :], local[:, q, t:t + 1],
                                               None, ALU.is_equal)
                    ins.then_inc(ends_done, 1)

                def slots(i, q, peeled):
                    g = i * 2 + q
                    m = slice(q * T, q * T + T)
                    if not peeled:
                        for t in range(T):
                            v.wait_ge(sent[q * T + t], i * 16)
                    vv.tensor_scalar(late[:, q, :], local[:, q, :], float(P - 1), float(1 << 22), ALU.is_gt, ALU.mult).then_inc(small, 1)
                    vv.tensor_copy(msg[:, m, D], meta[:, m, M_SRC]).then_inc(small, 1)
                    v.wait_ge(small, g * 3 + 1)
                    vv.tensor_tensor(slot[:, q, :], late[:, q, :], meta[:, m, M_SLOT], ALU.add).then_inc(small, 1)

                def tile(i, q, t, peeled):
                    u = q * T + t
                    n = i * (2 * T) + u
                    v.wait_ge(tile_done, n + 1)
                    vv.tensor_tensor(wgt[:, t, :], pW[:, u % 2, 0:D], b2[:, :], ALU.add).then_inc(biased, 1)
                    v.wait_ge(biased, n + 1)
                    if t == 0:
                        v.wait_ge(small, i * 6 + (q * 3 + 3))
                    vv.scalar_tensor_tensor(msg[:, u, 0:D], pW[:, u % 2, D:2 * D], meta[:, u, M_CUT:M_CUT + 1],
                                            wgt[:, t, :], ALU.mult, ALU.mult).then_inc(msg_done, 1)

                def turn(i, q, ahead1, peeled):
                    slots(i, q, peeled)
                    for t in range(T):
                        tile(i, q, t, peeled)
                        if ahead1 and t == 1:
                            find_ends(i + q, 1 - q, peeled and q == 0)
                        if ahead1 and t == 2:
                            hidden(i * 2 + (q + 1), 1 - q)

                v.wait_ge(sched, 48)
                v.wait_ge(const_in, 96)
                v.wait_ge(fill_out, 16)
                find_ends(0, 0, True)
                hidden(0, 0)
                for q in range(2):
                    turn(0, q, True, True)
                with v.Fori(1, G // 2 - 1) as i:
                    for q in range(2):
                        turn(i, q, True, False)
                for q in range(2):
                    turn(G // 2 - 1, q, q == 0, False)


def sum_phase(nc, io, S, keep):
    U = D_UNROLL
    accT = keep["accT"]
    with ExitStack() as ctx:
        sb, ps, sem = scope(nc, ctx)
        start = sb("d_start", [1, CS * P], I32)
        blk = sb("d_blk", [1, CS * P], I32)
        first = sb("d_first", [P, CS * P])
        msg = sb("d_msg", [P, U, 2, MSG])
        local = sb("d_local", [P, U, 2])
        mask = sb("d_mask", [P, U, 2, P])
        pD = ps("pD", [P, U, 512])
        sched = sem("d_sched")
        zeroed = sem("d_zeroed")
        msg_in = [sem(f"d_msg_in{u}") for u in range(U)]
        local_done = sem("d_local_done")
        mask_done = sem("d_mask_done")
        mult = sem("d_mult")
        added = sem("d_added")
        ITER = TILES_S // U

        with nc.Block() as block:
            @block.sync
            def _(sp):
                load_schedule(sp, S, 1, CS, start, blk, first, sched)
                sp.wait_ge(sched, 48)

                def body(i, peeled):
                    at = registers(nc, sp, start[0:1, bass.ds(i * U, U)], U, E)
                    for u in range(U):
                        if not peeled:
                            sp.wait_ge(mult, i * U + (u + 1 - U))
                        sp.dma_start(msg[:, u, :, :].rearrange("p j m -> p (j m)"),
                                     S["messages"][bass.ds(at[u], PAIR), :].rearrange("(p j) m -> p (j m)", j=2)
                                     ).then_inc(msg_in[u], 16)

                body(0, True)
                with sp.Fori(1, ITER) as i:
                    body(i, False)

            @block.gpsimd
            def _(pool):
                mid = NBLK // 2
                nc.gpsimd.memset(accT[:, mid:NBLK, :, :], 0.0).then_inc(zeroed, 1)

            @block.tensor
            def _(pe):
                def pair(i, u, peeled):
                    pe.wait_ge(msg_in[u], i * 16 + 16)
                    pe.wait_ge(mask_done, i * U + (u + 1))
                    if not peeled:
                        pe.wait_ge(added, i * U + (u + 1 - U))
                    for k in range(DK):
                        for j in range(2):
                            ins = nc.tensor.matmul(pD[:, u, k * P:(k + 1) * P], msg[:, u, j, k * P:(k + 1) * P],
                                                   mask[:, u, j, :], start=(j == 0), stop=(j == 1))
                    ins.then_inc(mult, 1)

                for u in range(U):
                    pair(0, u, True)
                with pe.Fori(1, ITER) as i:
                    for u in range(U):
                        pair(i, u, False)

            @block.vector
            def _(v):
                vv = nc.vector

                def locals_(i, u, peeled):
                    v.wait_ge(msg_in[u], i * 16 + 16)
                    vv.tensor_scalar(local[:, u, :], msg[:, u, :, D], first[:, bass.ds(i * U + u, 1)], None,
                                     ALU.subtract).then_inc(local_done, 1)

                def masks(i, u):
                    v.wait_ge(local_done, i * U + (u + 1))
                    for j in range(2):
                        ins = vv.tensor_scalar(mask[:, u, j, :], keep["iota_row"][:, :], local[:, u, j:j + 1],
                                               None, ALU.is_equal)
                    ins.then_inc(mask_done, 1)

                def add(i, u, at, peeled):
                    v.wait_ge(mult, i * U + (u + 1))
                    if not (peeled and u == 0):
                        v.wait_ge(added, i * U + u)
                    to = accT[:, bass.ds(at, 1), :, :].rearrange("p a k n -> p (a k n)")
                    vv.tensor_tensor(to, pD[:, u, 0:D], to, ALU.add).then_inc(added, 1)

                vv.memset(accT[:, 0:NBLK // 2, :, :], 0.0).then_inc(zeroed, 1)
                v.wait_ge(zeroed, 2)
                v.wait_ge(sched, 48)
                for u in range(U):
                    locals_(0, u, True)
                    masks(0, u)

                def body(i, ahead, peeled):
                    at = registers(nc, v, blk[0:1, bass.ds(i * U, U)], U, NBLK - 1)
                    for u in range(U):
                        add(i, u, at[u], peeled)
                        if ahead:
                            if u:
                                masks(i + 1, u - 1)
                            locals_(i + 1, u, False)
                    if ahead:
                        masks(i + 1, U - 1)

                body(0, True, True)
                with v.Fori(1, ITER - 1) as i:
                    body(i, True, False)
                body(ITER - 1, False, False)


def output_phase(nc, io, S, keep):
    x1, accT = keep["acc"], keep["accT"]
    with ExitStack() as ctx:
        sb, ps, sem = scope(nc, ctx)
        lin2 = sb("e_lin2", [P, DK, D])
        bias = sb("e_bias", [P, D])
        aggT = sb("e_aggT", [P, BU, DK, P])
        z = sb("e_z", [P, BU, D])
        soft = sb("e_soft", [P, BU, D])
        h = sb("e_h", [P, BU, D])
        stats = sb("e_stats", [P, BU, 6])
        mv = sb("e_mv", [P, BU, 2])
        mean = sb("e_mean", [P, NBLK])
        var = sb("e_var", [P, NBLK])
        std = sb("e_std", [P, NBLK])
        rstd = sb("e_rstd", [P, NBLK])
        eps = sb("e_eps", [P, 1])
        half_one = sb("e_half_one", [P, 1])
        out = sb("e_out", [P, BU, D])
        pE = ps("pE", [P, BU, 512])
        const_in = sem("e_const_in")
        consts = sem("e_consts")
        staged = sem("e_staged")
        mult = sem("e_mult")
        z_done = sem("e_z_done")
        soft_step = sem("e_soft_step")
        v_passed = sem("e_v_passed")
        dve = sem("e_dve")
        x2_done = sem("e_x2_done")
        std_done = sem("e_std_done")
        rstd_done = sem("e_rstd_done")
        out_done = sem("e_out_done")
        stored = [sem(f"e_stored{j}") for j in range(BU)]

        def at(a, b):
            return a[:, bass.ds(b, 1), :].rearrange("p a n -> p (a n)")

        with nc.Block() as block:
            @block.sync
            def _(sp):
                sp.dma_start(lin2[:, :, :], io["lin2"].rearrange("(k p) o -> p k o", p=P)).then_inc(const_in, 16)
                sp.dma_start(bias[:, :], io["lin2_b"].broadcast_to([P, D])).then_inc(const_in, 16)
                with sp.Fori(0, BI - 1) as i:
                    for j in range(BU):
                        sp.wait_ge(out_done, i * BU + (j + 1))
                        sp.dma_start(io["out"][bass.ds((i * BU + j) * P, P), :], out[:, j, :]).then_inc(stored[j], 16)
                for j in range(BU):
                    b = (BI - 1) * BU + j
                    rows = min(P, N - b * P)
                    sp.wait_ge(out_done, b + 1)
                    sp.dma_start(io["out"][b * P:b * P + rows, :], out[0:rows, j, :]).then_inc(stored[j], 16)
                for j in range(BU):
                    sp.wait_ge(stored[j], 16 * BI)

            @block.gpsimd
            def _(pool):
                g = nc.gpsimd
                g.memset(eps[:, :], 1e-5).then_inc(consts, 1)
                g.memset(half_one[:, :], 0.5).then_inc(consts, 1)

                def stage(i, j, peeled):
                    if not peeled:
                        pool.wait_ge(mult, i * BU + (j + 1 - BU))
                    g.tensor_copy(aggT[:, j, :, :].rearrange("p k n -> p (k n)"),
                                  accT[:, bass.ds(i * BU + j, 1), :, :].rearrange("p a k n -> p (a k n)")).then_inc(staged, 1)

                for j in range(BU):
                    stage(0, j, True)
                with pool.Fori(1, BI) as i:
                    for j in range(BU):
                        stage(i, j, False)

            @block.tensor
            def _(pe):
                def block_of(i, j, peeled):
                    pe.wait_ge(staged, i * BU + (j + 1))
                    if not peeled:
                        pe.wait_ge(z_done, i * BU + (j + 1 - BU))
                    for k in range(DK):
                        ins = nc.tensor.matmul(pE[:, j, 0:D], aggT[:, j, k, :], lin2[:, k, :],
                                               start=(k == 0), stop=(k == DK - 1))
                    ins.then_inc(mult, 1)

                pe.wait_ge(const_in, 32)
                for j in range(BU):
                    block_of(0, j, True)
                with pe.Fori(1, BI) as i:
                    for j in range(BU):
                        block_of(i, j, False)

            @block.scalar
            def _(act):
                def block_of(i, j, peeled):
                    n = i * BU + j
                    act.wait_ge(z_done, n + 1)
                    if not peeled:
                        act.wait_ge(x2_done, i * BU + (j + 1 - BU))
                    nc.scalar.activation(soft[:, j, :], z[:, j, :], ACT.Abs).then_inc(soft_step, 1)
                    act.wait_ge(soft_step, n * 3 + 1)
                    nc.scalar.activation(soft[:, j, :], soft[:, j, :], ACT.Exp, scale=-1.0).then_inc(soft_step, 1)
                    act.wait_ge(soft_step, n * 3 + 2)
                    nc.scalar.activation(soft[:, j, :], soft[:, j, :], ACT.Ln, scale=0.5, bias=half_one[:, :]).then_inc(soft_step, 1)

                nc.scalar.preload_act_table_set("natural_log_exp_and_others")
                act.wait_ge(consts, 2)
                for j in range(BU):
                    block_of(0, j, True)
                with act.Fori(1, BI) as i:
                    for j in range(BU):
                        block_of(i, j, False)
                act.wait_ge(x2_done, NBLK)
                nc.scalar.activation(std[:, :], var[:, :], ACT.Sqrt, bias=eps[:, :]).then_inc(std_done, 1)

            @block.vector
            def _(v):
                vv = nc.vector
                s = Steps(v, dve)

                def bias_of(i, j, peeled):
                    v.wait_ge(mult, i * BU + (j + 1))
                    if not peeled:
                        v.wait_ge(soft_step, i * (3 * BU) + (3 * j + 1 - 3 * BU))
                    vv.tensor_tensor(z[:, j, :], pE[:, j, 0:D], bias[:, :], ALU.add).then_inc(z_done, 1)

                def rest(i, j):
                    n = i * BU + j
                    v.wait_ge(soft_step, n * 3 + 3)
                    s.add(vv.scalar_tensor_tensor(h[:, j, :], z[:, j, :], 0.0, soft[:, j, :], ALU.max, ALU.add))
                    s.wait()
                    s.add(vv.scalar_tensor_tensor(at(x1, n), at(x1, n), 2.0, h[:, j, :], ALU.mult, ALU.add))
                    s.wait()
                    passed(v, v_passed)
                    s.add(vv.bn_stats(stats[:, j, :], at(x1, n)))
                    s.wait()
                    passed(v, v_passed)
                    s.add(vv.bn_aggr(mv[:, j, :], stats[:, j, :]))
                    s.wait()
                    s.add(vv.tensor_copy(mean[:, bass.ds(n, 1)], mv[:, j, 0:1]))
                    vv.tensor_copy(var[:, bass.ds(n, 1)], mv[:, j, 1:2]).then_inc(x2_done, 1)

                v.wait_ge(const_in, 32)
                for j in range(BU):
                    bias_of(0, j, True)
                with v.Fori(1, BI) as i:
                    s.loop(i, 1, 5 * BU)
                    for j in range(BU):
                        rest(i - 1, j)
                        bias_of(i, j, False)
                s.end(BI - 1)
                for j in range(BU):
                    rest(BI - 1, j)
                v.wait_ge(std_done, 1)
                vv.reciprocal(rstd[:, :], std[:, :]).then_inc(rstd_done, 1)
                v.wait_ge(rstd_done, 1)

                def norm(i, j, peeled):
                    n = i * BU + j
                    if not peeled:
                        v.wait_ge(stored[j], i * 16)
                    vv.tensor_scalar(out[:, j, :], at(x1, n), mean[:, bass.ds(n, 1)],
                                     rstd[:, bass.ds(n, 1)], ALU.subtract, ALU.mult).then_inc(out_done, 1)

                for j in range(BU):
                    norm(0, j, True)
                with v.Fori(1, BI) as i:
                    for j in range(BU):
                        norm(i, j, False)


def gnn_kernel(nc, io):
    with ExitStack() as ctx:
        sb, ps, sem = scope(nc, ctx)
        S = dict(
            table=nc.dram_tensor("table", [NBLK * P * REL, D], F32).ap(),
            records=nc.dram_tensor("records", [EP, META], F32).ap(),
            dst=nc.dram_tensor("sorted_dst", [EP, 1], F32).ap(),
            attr50=nc.dram_tensor("sorted_attr50", [EP, G50], F32).ap(),
            start=nc.dram_tensor("tile_start", [2, CD * P], I32).ap(),
            block=nc.dram_tensor("tile_block", [2, CD * P], I32).ap(),
            first_node=nc.dram_tensor("tile_first_node", [2, CD * P], F32).ap(),
            messages=nc.dram_tensor("messages", [E + PAIR, MSG], F32).ap())
        keep = dict(acc=sb("acc", [P, NBLK, D]), ident=sb("ident", [P, P]), iota_row=sb("iota_row", [P, P]))
        setup_phase(nc, io, S, keep)
        relation_phase(nc, io, S, keep)
        with nc.sbuf_tensor("y3", [P, NBLK, 3, D], BF16) as keep["y3"]:
            norm_phase(nc, io, S, keep)
            edge_phase(nc, io, S, keep)
        with nc.sbuf_tensor("accT", [P, NBLK, DK, P], F32) as keep["accT"]:
            sum_phase(nc, io, S, keep)
            output_phase(nc, io, S, keep)

def host_arrays(x, src, dst, edge_attr_3, edge_attr_50, edge_type_16, edge_weight1, L0_gnn_weight,
                L0_gnn_w_comp, L0_gnn_h_bias, L0_gnn_loop_weight, L1_gnn_mlp_w1, L1_gnn_mlp_b1,
                L1_gnn_mlp_w2, L1_gnn_mlp_b2, L1_gnn_lin1_w, L1_gnn_lin2_w, L1_gnn_lin2_b):
    import numpy as np

    def pad(a, rows, fill=0):
        a = np.asarray(a)
        out = np.full((rows,) + a.shape[1:], fill, a.dtype)
        out[:a.shape[0]] = a
        return out

    xp = pad(x, NBLK * P)
    return dict(
        x=xp,
        xT=np.ascontiguousarray(xp.reshape(NBLK, P, DK, P).transpose(0, 3, 2, 1)).reshape(NBLK, P, DK * P),
        src=pad(src, EP, PADNODE).reshape(P, EC), dst=pad(dst, EP, PADNODE).reshape(P, EC),
        etype=pad(edge_type_16, EP).reshape(P, EC), norm=pad(edge_weight1, EP).reshape(P, EC),
        attr3=pad(edge_attr_3, EP).reshape(P, EC * 3), attr50=pad(edge_attr_50, EP),
        weight=np.asarray(L0_gnn_weight), w_comp=np.asarray(L0_gnn_w_comp).reshape(1, REL * BASES),
        h_bias=np.asarray(L0_gnn_h_bias).reshape(1, D), loop_weight=np.asarray(L0_gnn_loop_weight),
        w1=np.asarray(L1_gnn_mlp_w1), b1=np.asarray(L1_gnn_mlp_b1).reshape(1, D),
        w2=np.asarray(L1_gnn_mlp_w2), b2=np.asarray(L1_gnn_mlp_b2).reshape(1, D),
        lin1=np.asarray(L1_gnn_lin1_w), lin2=np.asarray(L1_gnn_lin2_w),
        lin2_b=np.asarray(L1_gnn_lin2_b).reshape(1, D))


def kernel(**inputs):
    import numpy as np
    import concourse.bacc as bacc
    from concourse.bass_utils import run_bass_kernel_spmd

    nc = bacc.Bacc("TRN2", target_bir_lowering=False, num_devices=1)
    arrays = {f"in_{name}_dram": a for name, a in host_arrays(**inputs).items()}
    io = {name[3:-5]: nc.dram_tensor(name, a.shape, mybir.dt.from_np(a.dtype), kind="ExternalInput").ap()
          for name, a in arrays.items()}
    io["out"] = nc.dram_tensor("out_0_dram", (N, D), F32, kind="ExternalOutput").ap()
    gnn_kernel(nc, io)
    r = run_bass_kernel_spmd(nc, [arrays], core_ids=[0])
    return np.asarray(r.results[0]["out_0_dram"])
```

```python
import concourse.bass as bass
from concourse import mybir
from contextlib import ExitStack
import math

F32 = mybir.dt.float32
BF16 = mybir.dt.bfloat16
I32 = mybir.dt.int32
ALU = mybir.AluOpType
ACT = mybir.ActivationFunctionType
AXX = mybir.AxisListType.X

P = 128
N = 6250
D = 256
DK = D // P
E = 106250
REL = 16
BASES = 8
G50 = 50
NBLK = -(-N // P)
EC = -(-E // P) + 1
EP = P * EC
PADNODE = NBLK * P
META = 6
M_ROW, M_NORM, M_DST, M_SLOT, M_CUT, M_SRC = range(META)
MSG = D + 8

B_UNROLL = 16
TILES_D = -(-((E + NBLK * (P - 1)) // P) // B_UNROLL) * B_UNROLL
D_UNROLL = 8
PAIR = 2 * P
TILES_S = -(-((E + NBLK * (PAIR - 1)) // PAIR) // D_UNROLL) * D_UNROLL
CD = -(-TILES_D // P)
CS = -(-TILES_S // P)

BU = 7
BI = NBLK // BU
assert BU * BI == NBLK
CUTOFF = 2.0
HALF = P // 2


def passed(eng, sem):
    eng.sem_inc(sem, 1)


class Steps:

    def __init__(self, eng, sem):
        self.eng, self.sem, self.base, self.n = eng, sem, 0, 0

    def add(self, ins):
        self.n += 1
        ins.then_inc(self.sem, 1)
        return self.base + self.n

    def wait(self, value=None):
        self.eng.wait_ge(self.sem, self.base + self.n if value is None else value)

    def loop(self, i, first, per):
        self.start, self.per = self.base + self.n, per
        self.base, self.n = (i - first) * per + self.start, 0

    def end(self, count):
        assert self.n == self.per, (self.n, self.per)
        self.base, self.n = self.start + self.per * count, 0


def scope(nc, ctx):
    def sb(name, shape, dt=F32):
        return ctx.enter_context(nc.sbuf_tensor(name, shape, dt))

    def ps(name, shape, dt=F32):
        return ctx.enter_context(nc.psum_tensor(name, shape, dt))

    def sem(name):
        return ctx.enter_context(nc.semaphore(name))

    return sb, ps, sem


def registers(nc, eng, row, count, most):
    _, vals = nc.values_load_multi_w_load_instructions(
        row, engines=[eng.engine], min_val=0, max_val=most,
        skip_runtime_bounds_check_because="the schedule is clipped to the arrays when it is made")
    assert len(vals) == count
    return vals


def load_schedule(eng, S, k, cols, start, block, first, ready):
    eng.dma_start(start[:, :], S["start"][k:k + 1, 0:cols * P]).then_inc(ready, 16)
    eng.dma_start(block[:, :], S["block"][k:k + 1, 0:cols * P]).then_inc(ready, 16)
    eng.dma_start(first[:, :], S["first_node"][k:k + 1, 0:cols * P].broadcast_to([P, cols * P])).then_inc(ready, 16)


def setup_phase(nc, io, S, keep):
    with ExitStack() as ctx:
        sb, ps, sem = scope(nc, ctx)
        wb = sb("wb", [P, DK, BASES, D])
        wf = sb("wf", [P, DK, REL, D])
        comp = sb("comp", [P, REL * BASES])
        xt = sb("xt", [P, BU, DK, P])
        NU = 7
        outs = sb("outs", [P, NU, 2, 512])
        srci = sb("srci", [P, EC], I32)
        dsti = sb("dsti", [P, EC], I32)
        a3 = sb("a3", [P, EC, 3])
        keys = [sb("key_d", [P, EC]), sb("key_s", [P, EC])]
        pos = [sb("pos_d", [P, EC]), sb("pos_s", [P, EC])]
        meta = sb("meta", [P, EC, META])
        spare = wb[:, :, :, :].rearrange("p k b n -> p (k b n)")
        mask = [spare[:, k * EC:(k + 1) * EC] for k in range(2)]
        runs = [spare[:, k * EC:(k + 1) * EC] for k in range(2, 4)]
        eidx = sb("eidx", [P, EC])
        posi = sb("posi", [P, EC], I32)
        blki = posi
        typi, wgt = posi, keys[1]
        cut_a, cut_b, cut_m = pos[0], pos[1], keys[0]
        cnt, tot, cum, off, ntf, tend, padn = (spare[:, 4 * EC + k * 2 * NBLK:4 * EC + (k + 1) * 2 * NBLK]
                                               for k in range(7))
        assert 4 * EC + 14 * NBLK <= DK * BASES * D
        nti = sb("nti", [P, 2 * NBLK], I32)
        zer = sb("zer", [P, NBLK])
        iota49 = sb("iota49", [P, NBLK])
        iotac = [sb("iotac_d", [P, CD]), sb("iotac_s", [P, CS])]
        tri = sb("tri", [P, P])
        ones = sb("ones", [P, P])
        ident = keep["ident"]
        half_pi = sb("half_pi", [P, 1])
        flat3 = a3[:, :, :].rearrange("p c a -> p (c a)")
        ge = flat3[:, 0:CD * NBLK].rearrange("p (c b) -> p c b", b=NBLK)
        gep = flat3[:, CD * NBLK:2 * CD * NBLK].rearrange("p (c b) -> p c b", b=NBLK)
        sblk = [sb("sblk_d", [P, CD]), sb("sblk_s", [P, CS])]
        sbl128 = [sb("sbl128_d", [P, CD]), sb("sbl128_s", [P, CS])]
        sst = [sb("sst_d", [P, CD]), sb("sst_s", [P, CS])]
        sblki = [sb("sblki_d", [P, CD], I32), sb("sblki_s", [P, CS], I32)]
        ssti = [sb("ssti_d", [P, CD], I32), sb("ssti_s", [P, CS], I32)]
        moved = sb("moved", [P, 1])
        movedi = sb("movedi", [1, 1], I32)
        pA = ps("pA", [P, 8, 512])

        small_in = sem("small_in")
        edges_in = sem("edges_in")
        xt_in = [sem(f"xt_in{j}") for j in range(BU)]
        consts = sem("consts")
        dve_steps = sem("dve_steps")
        w_ready = sem("w_ready")
        pe_chunk = sem("pe_chunk")
        chunk_out = sem("chunk_out")
        stored = [sem(f"stored{u}") for u in range(NU)]
        act_cut = sem("act_cut")
        counted = sem("counted")
        pe_counts = sem("pe_counts")
        unsorted = sem("unsorted")
        pe_unsorted = sem("pe_unsorted")
        records = sem("records")
        schedule = sem("schedule")
        rec_out = sem("rec_out")
        sched_out = sem("sched_out")
        sched_in = sem("sched_in")
        copied = sem("copied")
        bases_in = sem("bases_in")
        cut_go = sem("cut_go")
        st_in = sem("st_in")
        st_copied = sem("st_copied")
        pool_passed = sem("a_pool_passed")
        st_out = [sem(f"st_out{q}") for q in range(2)]
        CONSTS = 12
        st_feat = sb("st_feat", [P, G50])
        st_meta = sb("st_meta", [P, META])
        st_pos = sb("st_pos", [P, 1], I32)

        def unit(i, h):
            return (h % BU, h // BU) if isinstance(i, int) and i == 0 else (h // 4, h % 4)

        with nc.Block() as block:

            @block.sync
            def _(sp):
                sp.dma_start(comp[:, :], io["w_comp"].broadcast_to([P, REL * BASES])).then_inc(small_in, 16)
                for k in range(DK):
                    sp.dma_start(wb[:, k, :, :], io["weight"][:, k * P:(k + 1) * P, :]
                                 .rearrange("b p o -> p b o")).then_inc(bases_in, 16)

                def load_x(blk, j):
                    sp.dma_start(xt[:, j, :, :], io["xT"][bass.ds(blk, 1)]
                                 .rearrange("a p (k n) -> (a p) k n", k=DK)).then_inc(xt_in[j], 16)

                for j in range(BU):
                    load_x(j, j)
                sp.dma_start(a3[:, :, :], io["attr3"].rearrange("p (c a) -> p c a", a=3)).then_inc(edges_in, 16)
                sp.dma_start(srci[:, :], io["src"]).then_inc(edges_in, 16)
                sp.dma_start(dsti[:, :], io["dst"]).then_inc(edges_in, 16)
                sp.dma_start(typi[:, :], io["etype"]).then_inc(edges_in, 16)
                sp.dma_start(wgt[:, :], io["norm"]).then_inc(edges_in, 16)

                def store(i, h):
                    slot = h % NU
                    j, part = unit(i, h)
                    sp.wait_ge(chunk_out, i * (8 * BU) + (2 * h + 2))
                    sp.dma_start(S["table"].rearrange("(n r) d -> n (r d)", r=REL)[
                        bass.ds((i * BU + j) * P, P), part * 1024:(part + 1) * 1024],
                        outs[:, slot, :, :].rearrange("p c n -> p (c n)")).then_inc(stored[slot], 16)

                for h in range(4 * BU):
                    store(0, h)
                    if h >= 3 * BU:
                        sp.wait_ge(pe_chunk, 2 * h + 2)
                        load_x(BU + h - 3 * BU, h - 3 * BU)
                with sp.Fori(2, BI) as i:
                    for j in range(BU):
                        for part in range(4):
                            store(i - 1, 4 * j + part)
                        sp.wait_ge(pe_chunk, i * (8 * BU) + 8 * (j + 1 - BU))
                        load_x(i * BU + j, j)
                for h in range(4 * BU):
                    store(BI - 1, h)
                for u in range(NU):
                    sp.wait_ge(stored[u], 16 * 4 * BI)

            @block.gpsimd
            def _(pool):
                g = nc.gpsimd
                c = Steps(pool, consts)
                c.add(g.iota(iota49[:, :], [[1, NBLK]], base=0, channel_multiplier=0, allow_small_or_imprecise_dtypes=True))
                for k, cols in enumerate((CD, CS)):
                    c.add(g.iota(iotac[k][:, :], [[1, cols]], base=0, channel_multiplier=cols, allow_small_or_imprecise_dtypes=True))
                c.add(g.iota(eidx[:, :], [[1, EC]], base=0, channel_multiplier=EC, allow_small_or_imprecise_dtypes=True))
                c.add(g.iota(keep["iota_row"][:, :], [[1, P]], base=0, channel_multiplier=0, allow_small_or_imprecise_dtypes=True))
                c.add(g.memset(ident[:, :], 0.0))
                c.add(g.memset(tri[:, :], 1.0))
                c.add(g.memset(ones[:, :], 1.0))
                c.add(g.memset(zer[:, :], 0.0))
                c.add(g.memset(half_pi[:, :], math.pi / 2))
                c.wait()
                c.add(g.affine_select(out=ident[:, :], in_=ident[:, :], compare_op=ALU.not_equal, fill=1.0,
                                      base=0, pattern=[[-1, P]], channel_multiplier=1))
                c.add(g.affine_select(out=tri[:, :], in_=tri[:, :], compare_op=ALU.is_gt, fill=0.0,
                                      base=0, pattern=[[1, P]], channel_multiplier=-1))
                assert c.n == CONSTS
                c.add(g.memset(keep["acc"][:, :, :], 0.0))
                pool.wait_ge(edges_in, 80)
                c.add(g.tensor_tensor(a3[:, :, :], a3[:, :, :], a3[:, :, :], ALU.mult))
                c.wait()
                c.add(g.tensor_tensor(cut_a[:, :], a3[:, :, 0], a3[:, :, 1], ALU.add))
                c.wait()
                g.tensor_tensor(cut_a[:, :], cut_a[:, :], a3[:, :, 2], ALU.add).then_inc(cut_go, 1)
                pool.wait_ge(act_cut, 1)
                g.tensor_scalar(cut_m[:, :], cut_b[:, :], CUTOFF, None, ALU.is_le).then_inc(cut_go, 1)
                g.tensor_scalar(cut_a[:, :], cut_b[:, :], CUTOFF, None, ALU.min).then_inc(cut_go, 1)
                pool.wait_ge(w_ready, REL // 2)
                PARTS, ROWS = 16, 52
                assert EP % (PARTS * ROWS) == 0
                per = EP // (PARTS * ROWS)
                gap = 8 * NBLK // PARTS
                with pool.Fori(0, PARTS) as a:
                    pool.wait_ge(pe_chunk, a * gap + 1)
                    pool.dma_start(S["attr50"].rearrange("(a r) c -> a (r c)", r=ROWS)[bass.ds(a * per, per), :],
                                   io["attr50"].rearrange("(a r) c -> a (r c)", r=ROWS)[bass.ds(a * per, per), :]).then_inc(copied, 16)
                pool.wait_ge(records, 1)
                pool.dma_start(S["records"].rearrange("(p c) m -> p (c m)", p=P),
                               meta[:, :, :].rearrange("p c m -> p (c m)")).then_inc(rec_out, 16)
                pool.wait_ge(schedule, 2)
                for k in range(2):
                    for to, of in ((S["start"], ssti), (S["block"], sblki), (S["first_node"], sbl128)):
                        cols = of[k].shape[1]
                        pool.dma_start(to[k:k + 1, 0:cols * P].rearrange("a (p c) -> p (a c)", p=P),
                                       of[k][:, :]).then_inc(sched_out, 16)
                pool.wait_ge(sched_out, 96)
                for k, cols in enumerate((CD, CS)):
                    load_schedule(pool, S, k, cols, *keep["sched"][k], sched_in)
                pool.wait_ge(sched_in, 96)
                pool.wait_ge(rec_out, 16)
                pool.wait_ge(copied, 16 * PARTS)

            @block.scalar
            def _(act):
                act.wait_ge(cut_go, 1)
                nc.scalar.activation(cut_b[:, :], cut_a[:, :], ACT.Sqrt).then_inc(act_cut, 1)

                def cosine():
                    act.wait_ge(cut_go, 3)
                    act.wait_ge(consts, CONSTS)
                    nc.scalar.activation(cut_b[:, :], cut_a[:, :], ACT.Sin, bias=half_pi[:, :],
                                         scale=-math.pi / (2 * CUTOFF)).then_inc(act_cut, 1)

                def chunks(i, first):
                    for h in range(4 * BU):
                        slot = h % NU
                        if first and h == NU:
                            cosine()
                        if not (first and h < NU):
                            act.wait_ge(stored[slot], i * 64 + 16 * (h // NU))
                        for q in range(2):
                            act.wait_ge(pe_chunk, i * (8 * BU) + (2 * h + q + 1))
                            nc.scalar.copy(outs[:, slot, q, :], pA[:, (2 * h + q) % 4, :]).then_inc(chunk_out, 1)

                chunks(0, True)
                with act.Fori(1, BI) as i:
                    chunks(i, False)

            @block.tensor
            def _(pe):
                def table_units(i, first):
                    for h in range(4 * BU):
                        j, part = unit(i, h)
                        if first and h < BU or not first and part == 0:
                            pe.wait_ge(xt_in[j], i * 16 + 16)
                        for q in range(2):
                            n, c = 2 * h + q, 2 * part + q
                            if first and j == 0:
                                pe.wait_ge(w_ready, c + 1)
                            if not (first and n < 4):
                                pe.wait_ge(chunk_out, i * (8 * BU) + (n - 3))
                            for k in range(DK):
                                ins = nc.tensor.matmul(pA[:, n % 4, :], xt[:, j, k, :],
                                                       wf[:, k, 2 * c:2 * c + 2, :].rearrange("p r n -> p (r n)"),
                                                       start=(k == 0), stop=(k == DK - 1))
                            ins.then_inc(pe_chunk, 1)

                for i in range(2):
                    table_units(i, i == 0)
                pe.wait_ge(consts, CONSTS)
                pe.wait_ge(counted, 1)
                nc.tensor.matmul(pA[:, 5, 0:2 * NBLK], ones[:, :], cnt[:, :], start=True, stop=True)
                nc.tensor.matmul(pA[:, 6, 0:2 * NBLK], tri[:, :], cnt[:, :], start=True, stop=True).then_inc(pe_counts, 1)
                with pe.Fori(2, BI) as i:
                    table_units(i, False)
                pe.wait_ge(unsorted, 1)
                nc.tensor.matmul(pA[0:1, 7, 0:1], moved[:, :], ones[:, 0:1], start=True, stop=True).then_inc(pe_unsorted, 1)

            @block.vector
            def _(v):
                vv = nc.vector
                s = Steps(v, dve_steps)
                v.wait_ge(small_in, 16)
                v.wait_ge(bases_in, 16 * DK)
                with v.Fori(0, REL // 2) as pair:
                    s.loop(pair, 0, 2 * (BASES - 1))
                    for b in range(BASES):
                        for a in range(2):
                            to = wf[:, :, bass.ds(pair * 2 + a, 1), :].rearrange("p k a n -> p k (a n)")
                            by = comp[:, bass.ds(pair * (2 * BASES) + (a * BASES + b), 1)]
                            if b == 0:
                                s.add(vv.tensor_scalar(to, wb[:, :, 0, :], by, None, ALU.mult))
                                continue
                            s.wait(s.base + 2 * b + a - 1)
                            ins = vv.scalar_tensor_tensor(to, wb[:, :, b, :], by, to, ALU.mult, ALU.add)
                            if b < BASES - 1:
                                s.add(ins)
                    ins.then_inc(w_ready, 1)
                s.end(REL // 2)
                v.wait_ge(edges_in, 80)
                s.add(vv.scalar_tensor_tensor(meta[:, :, M_ROW].bitcast(I32), srci[:, :], float(REL), typi[:, :],
                                              ALU.mult, ALU.add))
                s.wait()
                s.add(vv.tensor_scalar(meta[:, :, M_ROW].bitcast(I32), meta[:, :, M_ROW].bitcast(I32),
                                       float(NBLK * P * REL - 1), None, ALU.min))
                s.add(vv.tensor_copy(meta[:, :, M_NORM], wgt[:, :]))
                s.add(vv.tensor_copy(meta[:, :, M_DST], dsti[:, :]))
                s.add(vv.tensor_copy(meta[:, :, M_SRC], srci[:, :]))
                v.wait_ge(act_cut, 2)
                s.add(vv.tensor_tensor(cut_b[:, :], cut_b[:, :], cut_b[:, :], ALU.mult))
                s.wait()
                s.add(vv.tensor_tensor(meta[:, :, M_CUT], cut_b[:, :], cut_m[:, :], ALU.mult))
                v.wait_ge(consts, CONSTS)
                for k, of in enumerate((dsti, srci)):
                    s.wait()
                    s.add(vv.tensor_scalar(blki[:, :], of[:, :], 7, None, ALU.arith_shift_right))
                    s.wait()
                    s.add(vv.tensor_copy(keys[k][:, :], blki[:, :]))
                    s.wait()
                    s.add(vv.scalar_tensor_tensor(pos[k][:, :], keys[k][:, :], float(NBLK), eidx[:, :], ALU.is_equal, ALU.mult))
                with v.Fori(0, NBLK) as b:
                    s.loop(b, 0, 2)
                    for k in range(2):
                        s.wait(s.base + s.n - 1)
                        s.add(vv.tensor_scalar(mask[k], keys[k][:, :], iota49[:, bass.ds(b, 1)], None,
                                               ALU.is_equal, ALU.add, accum_out=cnt[:, bass.ds(b + k * NBLK, 1)]))
                s.end(NBLK)
                s.wait()
                vv.memset(moved[:, :], 0.0).then_inc(counted, 1)
                v.wait_ge(pe_counts, 1)
                s.add(vv.tensor_copy(tot[:, :], pA[:, 5, 0:2 * NBLK]))
                s.wait()
                for k in range(2):
                    h = slice(k * NBLK, (k + 1) * NBLK)
                    s.add(vv.tensor_tensor_scan(cum[:, h], tot[:, h], zer[:, :], 0.0, ALU.add, ALU.add))
                s.wait()
                s.add(vv.tensor_tensor(off[:, :], cum[:, :], tot[:, :], ALU.subtract))
                s.wait()
                s.add(vv.scalar_tensor_tensor(off[:, :], off[:, :], -1.0, pA[:, 6, 0:2 * NBLK], ALU.add, ALU.add))
                with v.Fori(0, NBLK) as b:
                    s.loop(b, 0, 8)
                    s.wait()
                    for k in range(2):
                        s.add(vv.tensor_scalar(mask[k], keys[k][:, :], iota49[:, bass.ds(b, 1)], None, ALU.is_equal))
                    for k in range(2):
                        s.wait(s.base + 1 + k)
                        s.add(vv.tensor_tensor_scan(runs[k], mask[k], mask[k],
                                                    off[:, bass.ds(b + k * NBLK, 1)], ALU.add, ALU.bypass))
                    for k in range(2):
                        s.wait(s.base + 3 + k)
                        s.add(vv.tensor_tensor(runs[k], runs[k], mask[k], ALU.mult))
                    for k in range(2):
                        s.wait(s.base + 5 + k)
                        s.add(vv.tensor_tensor(pos[k][:, :], pos[k][:, :], runs[k], ALU.add))
                s.end(NBLK)
                s.wait()
                vv.tensor_copy(meta[:, :, M_SLOT], pos[1][:, :]).then_inc(records, 1)
                s.add(vv.tensor_copy(posi[:, :], pos[0][:, :]))
                s.add(vv.tensor_tensor(mask[0], pos[0][:, :], eidx[:, :], ALU.not_equal))
                s.wait()
                vv.reduce_sum(moved[:, :], mask[0], AXX).then_inc(unsorted, 1)
                for k, (size, cols) in enumerate(((P, CD), (PAIR, CS))):
                    h = slice(k * NBLK, (k + 1) * NBLK)
                    s.add(vv.tensor_scalar(nti[:, h], tot[:, h], float(size - 1), None, ALU.add))
                    s.wait()
                    s.add(vv.tensor_scalar(nti[:, h], nti[:, h], size.bit_length() - 1, None, ALU.arith_shift_right))
                    s.wait()
                    s.add(vv.tensor_copy(ntf[:, h], nti[:, h]))
                    s.wait()
                    s.add(vv.tensor_tensor_scan(tend[:, h], ntf[:, h], zer[:, :], 0.0, ALU.add, ALU.add))
                    s.add(vv.scalar_tensor_tensor(padn[:, h], ntf[:, h], float(size), tot[:, h], ALU.mult, ALU.subtract))
                    s.wait()
                    both = [P, cols, NBLK]
                    s.add(vv.tensor_tensor(ge[:, 0:cols, :], iotac[k][:, :].rearrange("p (c a) -> p c a", a=1).broadcast_to(both),
                                           tend[:, h].rearrange("p (a b) -> p a b", a=1).broadcast_to(both), ALU.is_ge))
                    s.wait()
                    s.add(vv.tensor_tensor(gep[:, 0:cols, :], ge[:, 0:cols, :],
                                           padn[:, h].rearrange("p (a b) -> p a b", a=1).broadcast_to(both), ALU.mult))
                    s.add(vv.reduce_sum(sblk[k][:, :], ge[:, 0:cols, :], AXX))
                    s.wait()
                    s.add(vv.reduce_sum(sst[k][:, :], gep[:, 0:cols, :], AXX))
                    s.add(vv.tensor_scalar(sblk[k][:, :], sblk[k][:, :], float(NBLK - 1), None, ALU.min))
                    s.wait()
                    s.add(vv.scalar_tensor_tensor(sst[k][:, :], iotac[k][:, :], float(size), sst[k][:, :], ALU.mult, ALU.subtract))
                    s.add(vv.tensor_scalar(sbl128[k][:, :], sblk[k][:, :], float(P), None, ALU.mult))
                    s.add(vv.tensor_copy(sblki[k][:, :], sblk[k][:, :]))
                    s.wait()
                    vv.tensor_scalar(ssti[k][:, :], sst[k][:, :], float(E), None, ALU.min).then_inc(schedule, 1)
                v.wait_ge(pe_unsorted, 1)
                s.add(vv.tensor_copy(movedi[:, :], pA[0:1, 7, 0:1]))

        with nc.Block() as block_sort:

            @block_sort.gpsimd
            def _(pool):
                g = nc.gpsimd
                (flag,) = registers(nc, pool, movedi[0:1, 0:1], 1, EP)
                with pool.If(flag > 0):
                    with pool.Fori(0, EC) as c:
                        pool.dma_start(st_feat[:, :], io["attr50"].rearrange("(p c) m -> p (c m)", p=P)[
                            :, bass.ds(c * G50, G50)]).then_inc(st_in, 16)
                        g.tensor_copy(st_meta[:, :], meta[:, bass.ds(c, 1), :].rearrange("p a m -> p (a m)")).then_inc(st_copied, 1)
                        g.tensor_copy(st_pos[:, :], posi[:, bass.ds(c, 1)]).then_inc(st_copied, 1)
                        pool.wait_ge(st_copied, c * 2 + 2)
                        pool.wait_ge(st_in, c * 16 + 16)
                        passed(pool, pool_passed)
                        for q, (to, of) in enumerate((("attr50", st_feat), ("records", st_meta))):
                            g.indirect_dma_start(out=S[to], out_offset=bass.IndirectOffsetOnAxis(ap=st_pos[:, 0:1], axis=0),
                                                 in_=of[:, :], in_offset=None).then_inc(st_out[q], 16)
                        for q in range(2):
                            pool.wait_ge(st_out[q], c * 16 + 16)
                        passed(pool, pool_passed)
                with pool.Else():
                    g.memset(st_meta[:, :], 0.0)


def relation_phase(nc, io, S, keep):
    U, H = B_UNROLL, B_UNROLL // 2
    ITER = TILES_D // U
    NPS = 4
    assert ITER > NBLK + 1
    acc = keep["acc"]
    start, blk, first = keep["sched"][0]
    with ExitStack() as ctx:
        sb, ps, sem = scope(nc, ctx)
        xt = sb("b_xt", [P, DK, P])
        loopw = sb("b_loopw", [P, DK, D])
        meta = sb("b_meta", [P, U, META])
        rows = sb("b_rows", [P, U, D])
        local = sb("b_local", [P, U])
        mask = sb("b_mask", [P, U, P])
        pB = ps("pB", [P, NPS, 512])
        pL = ps("pL", [P, 512])
        meta_in = [sem(f"b_meta_in{h}") for h in range(2)]
        rows_in = [sem(f"b_rows_in{u}") for u in range(U)]
        local_done = sem("b_local_done")
        mask_done = sem("b_mask_done")
        pool_passed = sem("b_pool_passed")
        mult = sem("b_mult")
        added = sem("b_added")
        loopw_in = sem("b_loopw_in")
        xt_in = sem("b_xt_in")
        loop_mult = sem("b_loop_mult")
        loop_added = sem("b_loop_added")
        later_in = sem("b_later_in")

        with nc.Block() as block:
            @block.sync
            def _(sp):
                def half(i, h, peeled):
                    at = registers(nc, sp, start[0:1, bass.ds(i * U + h * H, H)], H, E)
                    for u in range(H):
                        if not peeled:
                            sp.wait_ge(mult, i * U + (h * H + u + 1 - U))
                        sp.dma_start(meta[:, h * H + u, :], S["records"][bass.ds(at[u], P), :]).then_inc(meta_in[h], 16)

                def load_x(i):
                    sp.dma_start(xt[:, :, :], io["xT"][bass.ds(i, 1)].rearrange("a p (k n) -> (a p) k n", k=DK)).then_inc(xt_in, 16)

                for h in range(2):
                    half(0, h, True)
                sp.dma_start(loopw[:, :, :], io["loop_weight"].rearrange("(k p) o -> p k o", p=P)).then_inc(loopw_in, 16)
                load_x(0)
                later = [(keep["lin1"][:, :, :], io["lin1"].rearrange("(k p) o -> p k o", p=P)),
                         (keep["lin2"][:, :, :], io["lin2"].rearrange("(k p) o -> p k o", p=P)),
                         (keep["w2"][:, :, :], io["w2"].rearrange("(k p) o -> p k o", p=P)),
                         (keep["h_bias"][:, :], io["h_bias"].broadcast_to([P, D])),
                         (keep["b2"][:, :], io["b2"].broadcast_to([P, D])),
                         (keep["lin2_b"][:, :], io["lin2_b"].broadcast_to([P, D]))]
                for k in range(DK):
                    later.append((keep["w1"][k * HALF:k * HALF + G50, :], io["w1"][:, k * P:(k + 1) * P]))
                    later.append((keep["w1"][k * HALF + G50:k * HALF + G50 + 1, :], io["b1"][:, k * P:(k + 1) * P]))
                for to, of in later:
                    sp.dma_start(to, of).then_inc(later_in, 16)
                with sp.Fori(1, NBLK) as i:
                    for h in range(2):
                        half(i, h, False)
                    sp.wait_ge(loop_mult, i)
                    load_x(i)
                with sp.Fori(NBLK, ITER) as i:
                    for h in range(2):
                        half(i, h, False)
                sp.wait_ge(later_in, 16 * len(later))

            @block.gpsimd
            def _(pool):
                def half(i, h, peeled):
                    pool.wait_ge(meta_in[h], i * (16 * H) + 16 * H)
                    for u in range(h * H, h * H + H):
                        if not peeled:
                            pool.wait_ge(mult, i * U + (u + 1 - U))
                        passed(pool, pool_passed)
                        nc.gpsimd.indirect_dma_start(
                            out=rows[:, u, :], out_offset=None, in_=S["table"],
                            in_offset=bass.IndirectOffsetOnAxis(ap=meta[:, u, M_ROW:M_ROW + 1].bitcast(I32), axis=0),
                        ).then_inc(rows_in[u], 16)

                for h in range(2):
                    half(0, h, True)
                with pool.Fori(1, ITER) as i:
                    for h in range(2):
                        half(i, h, False)

            @block.tensor
            def _(pe):
                def tile(i, u, peeled):
                    if not (peeled and u < NPS):
                        pe.wait_ge(added, i * U + (u + 1 - NPS))
                    pe.wait_ge(mask_done, i * U + (u + 1))
                    pe.wait_ge(rows_in[u], i * 16 + 16)
                    nc.tensor.matmul(pB[:, u % NPS, 0:D], mask[:, u, :], rows[:, u, :],
                                     start=True, stop=True).then_inc(mult, 1)

                def loop_block(i, peeled):
                    pe.wait_ge(xt_in, i * 16 + 16)
                    if not peeled:
                        pe.wait_ge(loop_added, i)
                    for k in range(DK):
                        ins = nc.tensor.matmul(pL[:, 0:D], xt[:, k, :], loopw[:, k, :], start=(k == 0), stop=(k == DK - 1))
                    ins.then_inc(loop_mult, 1)

                for u in range(U):
                    tile(0, u, True)
                pe.wait_ge(loopw_in, 16)
                loop_block(0, True)
                with pe.Fori(1, NBLK) as i:
                    for u in range(U):
                        tile(i, u, False)
                    loop_block(i, False)
                with pe.Fori(NBLK, ITER) as i:
                    for u in range(U):
                        tile(i, u, False)

            @block.vector
            def _(v):
                vv = nc.vector

                def masks(i, h, peeled):
                    v.wait_ge(meta_in[h], i * (16 * H) + 16 * H)
                    if not peeled:
                        v.wait_ge(mult, i * U + (h * H + H - U))
                    u0 = h * H
                    vv.tensor_tensor(local[:, u0:u0 + H], meta[:, u0:u0 + H, M_DST],
                                     first[:, bass.ds(i * U + u0, H)], ALU.subtract).then_inc(local_done, 1)
                    v.wait_ge(local_done, i * 2 + (h + 1))
                    for u in range(u0, u0 + H):
                        vv.tensor_scalar(mask[:, u, :], keep["iota_row"][:, :], local[:, u:u + 1],
                                         meta[:, u, M_NORM:M_NORM + 1], ALU.is_equal, ALU.mult).then_inc(mask_done, 1)

                def adds(i, h, peeled):
                    at = registers(nc, v, blk[0:1, bass.ds(i * U + h * H, H)], H, NBLK - 1)
                    for u in range(H):
                        t = h * H + u
                        v.wait_ge(mult, i * U + (t + 1))
                        if not (peeled and t == 0):
                            v.wait_ge(added, i * U + t)
                        to = acc[:, bass.ds(at[u], 1), :].rearrange("p a n -> p (a n)")
                        vv.tensor_tensor(to, pB[:, t % NPS, 0:D], to, ALU.add).then_inc(added, 1)

                def add_loop(i):
                    v.wait_ge(loop_mult, i)
                    v.wait_ge(added, i * U)
                    to = acc[:, bass.ds(i - 1, 1), :].rearrange("p a n -> p (a n)")
                    vv.tensor_tensor(to, pL[:, 0:D], to, ALU.add).then_inc(loop_added, 1)

                def body(i, with_loop):
                    masks(i, 0, False)
                    adds(i - 1, 1, False)
                    if with_loop:
                        add_loop(i)
                    masks(i, 1, False)
                    if with_loop:
                        v.wait_ge(loop_added, i)
                    adds(i, 0, False)

                masks(0, 0, True)
                masks(0, 1, True)
                adds(0, 0, True)
                with v.Fori(1, NBLK + 1) as i:
                    body(i, True)
                with v.Fori(NBLK + 1, ITER) as i:
                    body(i, False)
                adds(ITER - 1, 1, False)


def norm_phase(nc, io, S, keep):
    acc = keep["acc"]
    y3 = keep["y3"]
    with ExitStack() as ctx:
        sb, ps, sem = scope(nc, ctx)
        bias, lin1 = keep["h_bias"], keep["lin1"]
        xin = sb("t_x", [P, BU, D])
        h = sb("t_h", [P, BU, D])
        stats = sb("t_stats", [P, BU, 6])
        mv = sb("t_mv", [P, BU, 2])
        eps = sb("t_eps", [P, 1])
        std = sb("t_std", [P, BU])
        rstd = sb("t_rstd", [P, BU])
        x1 = sb("t_x1", [P, BU, D])
        x1T = sb("t_x1T", [P, BU, DK, P])
        rest = sb("t_rest", [P, BU, D])
        pX = ps("pX", [P, 512])
        pY = ps("pY", [P, BU, 512])
        x_in = [sem(f"t_x_in{j}") for j in range(BU)]
        v_passed = sem("t_v_passed")
        dve = sem("t_dve")
        h_done = sem("t_h_done")
        std_go = sem("t_std_go")
        std_done = sem("t_std_done")
        x1_done = sem("t_x1_done")
        x1_kept = sem("t_x1_kept")
        turned = sem("t_turned")
        x1T_done = sem("t_x1T_done")
        y_done = sem("t_y_done")
        y_hi = sem("t_y_hi")
        y_all = sem("t_y_all")

        def at(a, b, *mid):
            return a[(slice(None), bass.ds(b, 1)) + mid]

        with nc.Block() as block:
            @block.sync
            def _(sp):
                for j in range(BU):
                    sp.dma_start(xin[:, j, :], io["x"][j * P:(j + 1) * P, :]).then_inc(x_in[j], 16)
                with sp.Fori(1, BI) as i:
                    for j in range(BU):
                        sp.wait_ge(h_done, i * BU + (j + 1 - BU))
                        sp.dma_start(xin[:, j, :], io["x"][bass.ds((i * BU + j) * P, P), :]).then_inc(x_in[j], 16)

            @block.gpsimd
            def _(pool):
                with pool.Fori(0, BI) as i:
                    for j in range(BU):
                        pool.wait_ge(x1_done, i * BU + (j + 1))
                        nc.gpsimd.tensor_copy(at(acc, i * BU + j).rearrange("p a n -> p (a n)"), x1[:, j, :]).then_inc(x1_kept, 1)

            @block.vector
            def _(v):
                vv = nc.vector
                s = Steps(v, dve)
                s.add(vv.memset(eps[:, :], 1e-5))

                def norm(i, peeled):
                    n = s.n
                    for j in range(BU):
                        if not peeled:
                            v.wait_ge(x1_done, i * BU + (j + 1 - BU))
                        s.add(vv.tensor_tensor(h[:, j, :], at(acc, i * BU + j).rearrange("p a n -> p (a n)"), bias[:, :], ALU.add))
                    for j in range(BU):
                        s.wait(s.base + n + j + 1)
                        v.wait_ge(x_in[j], i * 16 + 16)
                        vv.scalar_tensor_tensor(h[:, j, :], h[:, j, :], 0.0, xin[:, j, :], ALU.max, ALU.add).then_inc(h_done, 1)
                    v.wait_ge(h_done, i * BU + BU)
                    passed(v, v_passed)
                    for j in range(BU):
                        s.add(vv.bn_stats(stats[:, j, :], h[:, j, :]))
                    s.wait()
                    passed(v, v_passed)
                    for j in range(BU):
                        ins = vv.bn_aggr(mv[:, j, :], stats[:, j, :])
                    ins.then_inc(std_go, 1)

                def parts(i):
                    n = s.n
                    hi, mid, lo = ([y3[:, bass.ds(i * BU + j, 1), q, :].rearrange("p a n -> p (a n)") for j in range(BU)]
                                   for q in range(3))
                    for j in range(BU):
                        v.wait_ge(y_hi, i * BU + (j + 1))
                        s.add(vv.tensor_tensor(rest[:, j, :], pY[:, j, 0:D], hi[j], ALU.subtract))
                    for j in range(BU):
                        s.wait(s.base + n + j + 1)
                        s.add(vv.tensor_copy(mid[j], rest[:, j, :]))
                    for j in range(BU):
                        s.wait(s.base + n + BU + j + 1)
                        vv.tensor_tensor(lo[j], rest[:, j, :], mid[j], ALU.subtract).then_inc(y_all, 1)

                def apply(i, peeled):
                    v.wait_ge(std_done, i + 1)
                    s.add(vv.reciprocal(rstd[:, :], std[:, :]))
                    s.wait()
                    for j in range(BU):
                        if not peeled:
                            v.wait_ge(x1_kept, i * BU + (j + 1 - BU))
                            v.wait_ge(turned, i * BU + (j + 1 - BU))
                        vv.tensor_scalar(x1[:, j, :], h[:, j, :], mv[:, j, 0:1], rstd[:, j:j + 1],
                                         ALU.subtract, ALU.mult).then_inc(x1_done, 1)

                norm(0, True)
                apply(0, True)
                with v.Fori(1, BI) as i:
                    s.loop(i, 1, 4 * BU + 1)
                    norm(i, False)
                    parts(i - 1)
                    apply(i, False)
                s.end(BI - 1)
                parts(BI - 1)

            @block.scalar
            def _(act):
                def keep_turned(i, j, peeled):
                    act.wait_ge(turned, i * BU + (j + 1))
                    if not peeled:
                        act.wait_ge(y_done, i * BU + (j + 1 - BU))
                    nc.scalar.copy(x1T[:, j, :, :].rearrange("p k n -> p (k n)"), pX[:, 0:D]).then_inc(x1T_done, 1)

                def high(i, j):
                    act.wait_ge(y_done, i * BU + (j + 1))
                    nc.scalar.copy(y3[:, bass.ds(i * BU + j, 1), 0, :].rearrange("p a n -> p (a n)"),
                                   pY[:, j, 0:D]).then_inc(y_hi, 1)

                def body(i, peeled):
                    act.wait_ge(std_go, i + 1)
                    nc.scalar.activation(std[:, :], mv[:, :, 1], ACT.Sqrt, bias=eps[:, :]).then_inc(std_done, 1)
                    for j in range(BU):
                        keep_turned(i, j, peeled)
                        if j:
                            high(i, j - 1)
                    high(i, BU - 1)

                act.wait_ge(dve, 1)
                body(0, True)
                with act.Fori(1, BI) as i:
                    body(i, False)

            @block.tensor
            def _(pe):
                def turn(i, j, peeled):
                    pe.wait_ge(x1_done, i * BU + (j + 1))
                    if not (peeled and j == 0):
                        pe.wait_ge(x1T_done, i * BU + j)
                    for k in range(DK):
                        ins = nc.tensor.transpose(pX[:, k * P:(k + 1) * P], x1[:, j, k * P:(k + 1) * P], keep["ident"][:, :])
                    ins.then_inc(turned, 1)

                def multiply(i, j, peeled):
                    pe.wait_ge(x1T_done, i * BU + (j + 1))
                    if not peeled:
                        pe.wait_ge(y_all, i * BU + (j + 1 - BU))
                    for k in range(DK):
                        ins = nc.tensor.matmul(pY[:, j, 0:D], x1T[:, j, k, :], lin1[:, k, :],
                                               start=(k == 0), stop=(k == DK - 1))
                    ins.then_inc(y_done, 1)

                def body(i, peeled):
                    turn(i, 0, peeled)
                    for j in range(BU):
                        if j + 1 < BU:
                            turn(i, j + 1, peeled and j + 1 == 0)
                        multiply(i, j, peeled)

                body(0, True)
                with pe.Fori(1, BI) as i:
                    body(i, False)


def edge_phase(nc, io, S, keep):
    T = 4
    G = TILES_D // T
    KA = G50 + 1
    y3, ident = keep["y3"], keep["ident"]
    with ExitStack() as ctx:
        sb, ps, sem = scope(nc, ctx)
        start, blk, first = keep["sched"][0]
        w1, w2, b2 = keep["w1"], keep["w2"], keep["b2"]
        ident_b = sb("c_ident_b", [P, P], BF16)
        half_one = sb("c_half_one", [P, 1])
        feat = sb("c_feat", [P, 2 * T, 2, HALF])
        meta = sb("c_meta", [P, 2 * T, META])
        ends = sb("c_ends", [P, 2 * T, P], BF16)
        pick = sb("c_pick", [P, 2, T * P], BF16)
        local = sb("c_local", [P, 2, T])
        late = sb("c_late", [P, 2, T])
        cut = sb("c_cut", [P, 2, T])
        slot = sb("c_slot", [P, 2, T], I32)
        featT = sb("c_featT", [P, 2, T * P])
        soft = sb("c_soft", [P, 2, DK, T * P])
        hid = sb("c_hid", [P, 2, DK, T * P])
        wgt = sb("c_wgt", [P, T, D])
        msg = sb("c_msg", [P, 2 * T, MSG])
        pT = ps("pT", [P, 512])
        pP = ps("pP", [P, 1024], BF16)
        pH = ps("pH", [P, 2, DK, 512])
        pW = ps("pW", [P, 2, 512])

        pool_passed = sem("c_pool_passed")
        pe_passed = sem("c_pe_passed")
        sp_passed = sem("c_sp_passed")
        consts = sem("c_consts")
        fill_out = sem("c_fill_out")
        feat_in = [sem(f"c_feat_in{q}") for q in range(2)]
        meta_in = [sem(f"c_meta_in{q}") for q in range(2)]
        twice = sem("c_twice")
        turned = sem("c_turned")
        featT_done = sem("c_featT_done")
        layer1 = sem("c_layer1")
        soft_step = sem("c_soft_step")
        hid_done = sem("c_hid_done")
        ends_done = sem("c_ends_done")
        ends_turned = sem("c_ends_turned")
        pick_done = sem("c_pick_done")
        tile_done = sem("c_tile_done")
        biased = sem("c_biased")
        local_done = sem("c_local_done")
        small = sem("c_small")
        msg_done = sem("c_msg_done")
        sent = [sem(f"c_sent{u}") for u in range(2 * T)]

        with nc.Block() as block:
            @block.sync
            def _(sp):
                def feats(g, q):
                    at = registers(nc, sp, start[0:1, bass.ds(g * T, T)], T, E)
                    for t in range(T):
                        sp.dma_start(feat[:, q * T + t, 0, 0:G50], S["attr50"][bass.ds(at[t], P), :]).then_inc(feat_in[q], 16)

                def metas(g, q):
                    passed(sp, sp_passed)
                    at = registers(nc, sp, start[0:1, bass.ds(g * T, T)], T, E)
                    for t in range(T):
                        sp.dma_start(meta[:, q * T + t, :], S["records"][bass.ds(at[t], P), :]).then_inc(meta_in[q], 16)

                def turn(i, q, feats_ahead, metas_ahead):
                    g = i * 2 + q
                    if feats_ahead:
                        sp.wait_ge(turned, g + 2)
                        feats(g + 3, 1 - q)
                    if metas_ahead:
                        sp.wait_ge(small, g * 4 + 4)
                        metas(g + 2, q)

                feats(0, 0)
                metas(0, 0)
                feats(1, 1)
                metas(1, 1)
                sp.wait_ge(consts, 5)
                sp.dma_start(S["messages"][E:E + PAIR, :].rearrange("(p j) m -> p (j m)", j=2),
                             msg[:, 0:2, :].rearrange("p j m -> p (j m)")).then_inc(fill_out, 16)
                sp.wait_ge(turned, 1)
                feats(2, 0)
                with sp.Fori(0, G // 2 - 2) as i:
                    for q in range(2):
                        turn(i, q, True, True)
                for g in range(G - 4, G):
                    turn(g // 2, g % 2, g + 3 < G, g + 2 < G)
                sp.wait_ge(fill_out, 16)

            @block.gpsimd
            def _(pool):
                g_ = nc.gpsimd
                g_.memset(msg[:, :, :], 0.0).then_inc(consts, 1)
                g_.tensor_copy(ident_b[:, :], ident[:, :]).then_inc(consts, 1)
                g_.memset(half_one[:, :], 0.5).then_inc(consts, 1)
                pool.wait_ge(consts, 3)
                g_.memset(msg[:, 0:2, D], float(PADNODE)).then_inc(consts, 1)
                g_.memset(feat[:, :, :, G50:HALF], 1.0).then_inc(consts, 1)

                def tile(i, u):
                    pool.wait_ge(msg_done, i * (2 * T) + (u + 1))
                    passed(pool, pool_passed)
                    g_.indirect_dma_start(
                        out=S["messages"], out_offset=bass.IndirectOffsetOnAxis(ap=slot[:, u // T, u % T:u % T + 1], axis=0),
                        in_=msg[:, u, :], in_offset=None, bounds_check=E - 1, oob_is_err=False).then_inc(sent[u], 16)

                with pool.Fori(0, G // 2) as i:
                    for u in range(2 * T):
                        tile(i, u)
                for u in range(2 * T):
                    pool.wait_ge(sent[u], 16 * (G // 2))

            @block.tensor
            def _(pe):
                def turn_features(g, i, q, peeled):
                    pe.wait_ge(twice, g + 1)
                    if not peeled:
                        pe.wait_ge(featT_done, g)
                    passed(pe, pe_passed)
                    for t in range(T):
                        ins = nc.tensor.transpose(pT[:, t * P:(t + 1) * P],
                                                  feat[:, q * T + t, :, :].rearrange("p a c -> p (a c)"), ident[:, :])
                    ins.then_inc(turned, 1)

                def turn_ends(g, q, peeled):
                    pe.wait_ge(ends_done, g + 1)
                    if not peeled:
                        pe.wait_ge(pick_done, g)
                    passed(pe, pe_passed)
                    for t in range(T):
                        ins = nc.tensor.transpose(pP[:, t * P:(t + 1) * P], ends[:, q * T + t, :], ident_b[:, :])
                    ins.then_inc(ends_turned, 1)

                def first_layer(g, q, peeled):
                    pe.wait_ge(featT_done, g + 1)
                    if not peeled:
                        pe.wait_ge(hid_done, g - 1)
                    for k in range(DK):
                        rows = slice(k * HALF, k * HALF + KA)
                        ins = nc.tensor.matmul(pH[:, q, k, :], w1[rows, :], featT[rows, q, :], start=True, stop=True)
                    ins.then_inc(layer1, 1)

                def tiles(i, q, at, ahead1, peeled):
                    for t in range(T):
                        u = q * T + t
                        n = i * (2 * T) + u
                        if not (peeled and u < 2):
                            pe.wait_ge(msg_done, n - 1)
                        if t == 0:
                            pe.wait_ge(pick_done, i * 2 + (q + 1))
                        for part in range(3):
                            nc.tensor.matmul(pW[:, u % 2, D:2 * D], pick[:, q, t * P:(t + 1) * P],
                                             y3[:, bass.ds(at[t], 1), part, :].rearrange("p a n -> p (a n)"),
                                             start=(part == 0), stop=(part == 2))
                        if t == 0:
                            pe.wait_ge(hid_done, i * 2 + (q + 1))
                        for k in range(DK):
                            ins = nc.tensor.matmul(pW[:, u % 2, 0:D], hid[:, q, k, t * P:(t + 1) * P], w2[:, k, :],
                                                   start=(k == 0), stop=(k == DK - 1))
                        ins.then_inc(tile_done, 1)
                        if ahead1 and t == 2:
                            turn_ends(i * 2 + (q + 1), 1 - q, False)

                def turn(i, q, ahead1, ahead2, peeled):
                    g = i * 2 + q
                    if ahead1:
                        first_layer(g + 1, 1 - q, peeled and q == 0)
                    at = registers(nc, pe, blk[0:1, bass.ds(i * (2 * T) + q * T, T)], T, NBLK - 1)
                    if ahead2:
                        turn_features(g + 2, i + 1, q, False)
                    tiles(i, q, at, ahead1, peeled)

                pe.wait_ge(consts, 5)
                turn_features(0, 0, 0, True)
                first_layer(0, 0, True)
                turn_features(1, 0, 1, False)
                turn_ends(0, 0, True)
                for q in range(2):
                    turn(0, q, True, True, True)
                with pe.Fori(1, G // 2 - 1) as i:
                    for q in range(2):
                        turn(i, q, True, True, False)
                for q in range(2):
                    turn(G // 2 - 1, q, q == 0, False, False)

            @block.scalar
            def _(act):
                def soft_plus(i, q, g, step, peeled):
                    u = soft[:, q, :, :].rearrange("p k n -> p (k n)")
                    if step == 0:
                        act.wait_ge(layer1, g + 1)
                        if not peeled:
                            act.wait_ge(hid_done, g - 1)
                        nc.scalar.activation(u, pH[:, q, :, :].rearrange("p k n -> p (k n)"), ACT.Abs).then_inc(soft_step, 1)
                    elif step == 1:
                        act.wait_ge(soft_step, g * 3 + 1)
                        nc.scalar.activation(u, u, ACT.Exp, scale=-1.0).then_inc(soft_step, 1)
                    else:
                        act.wait_ge(soft_step, g * 3 + 2)
                        nc.scalar.activation(u, u, ACT.Ln, scale=0.5, bias=half_one[:, :]).then_inc(soft_step, 1)

                def copy_features(i, q):
                    act.wait_ge(feat_in[q], i * (16 * T) + 16 * T)
                    m = slice(q * T, q * T + T)
                    nc.scalar.copy(feat[:, m, 1, 0:G50], feat[:, m, 0, 0:G50]).then_inc(twice, 1)

                def keep_features(g, q, peeled):
                    act.wait_ge(turned, g + 1)
                    if not peeled:
                        act.wait_ge(layer1, g - 1)
                    nc.scalar.copy(featT[:, q, :], pT[:, :]).then_inc(featT_done, 1)

                def keep_picks(g, q, peeled):
                    act.wait_ge(ends_turned, g + 1)
                    if not peeled:
                        act.wait_ge(tile_done, (g - 1) * T)
                    nc.scalar.copy(pick[:, q, :], pP[:, 0:T * P]).then_inc(pick_done, 1)

                def turn(i, q, ahead1, ahead2, peeled):
                    g = i * 2 + q
                    if ahead2:
                        copy_features(i + 1, q)
                    if ahead1:
                        for step in range(2):
                            soft_plus(None, 1 - q, g + 1, step, peeled and q == 0)
                    if ahead2:
                        keep_features(g + 2, q, False)
                    if ahead1:
                        soft_plus(None, 1 - q, g + 1, 2, peeled and q == 0)
                        keep_picks(g + 1, 1 - q, peeled and q == 0)

                nc.scalar.preload_act_table_set("natural_log_exp_and_others")
                act.wait_ge(consts, 3)
                copy_features(0, 0)
                copy_features(0, 1)
                keep_features(0, 0, True)
                for step in range(3):
                    soft_plus(0, 0, 0, step, True)
                keep_features(1, 1, True)
                keep_picks(0, 0, True)
                for q in range(2):
                    turn(0, q, True, True, True)
                with act.Fori(1, G // 2 - 1) as i:
                    for q in range(2):
                        turn(i, q, True, True, False)
                for q in range(2):
                    turn(G // 2 - 1, q, q == 0, False, False)

            @block.vector
            def _(v):
                vv = nc.vector

                def hidden(g, q):
                    v.wait_ge(soft_step, g * 3 + 3)
                    vv.scalar_tensor_tensor(hid[:, q, :, :].rearrange("p k n -> p (k n)"),
                                            pH[:, q, :, :].rearrange("p k n -> p (k n)"), 0.0,
                                            soft[:, q, :, :].rearrange("p k n -> p (k n)"), ALU.max, ALU.add).then_inc(hid_done, 1)

                def find_ends(i, q, peeled):
                    g = i * 2 + q
                    m = slice(q * T, q * T + T)
                    v.wait_ge(meta_in[q], i * (16 * T) + 16 * T)
                    vv.tensor_tensor(local[:, q, :], meta[:, m, M_DST], first[:, bass.ds(g * T, T)], ALU.subtract).then_inc(local_done, 1)
                    v.wait_ge(local_done, g + 1)
                    if not peeled:
                        v.wait_ge(ends_turned, g - 1)
                    for t in range(T):
                        ins = vv.tensor_scalar(ends[:, q * T + t, :], keep["iota_row"][:, :], local[:, q, t:t + 1],
                                               None, ALU.is_equal)
                    ins.then_inc(ends_done, 1)

                def slots(i, q, peeled):
                    g = i * 2 + q
                    m = slice(q * T, q * T + T)
                    if not peeled:
                        for t in range(T):
                            v.wait_ge(sent[q * T + t], i * 16)
                    vv.tensor_scalar(late[:, q, :], local[:, q, :], float(P - 1), float(1 << 22), ALU.is_gt, ALU.mult).then_inc(small, 1)
                    vv.tensor_copy(msg[:, m, D], meta[:, m, M_SRC]).then_inc(small, 1)
                    vv.tensor_copy(cut[:, q, :], meta[:, m, M_CUT]).then_inc(small, 1)
                    v.wait_ge(small, g * 4 + 1)
                    vv.tensor_tensor(slot[:, q, :], late[:, q, :], meta[:, m, M_SLOT], ALU.add).then_inc(small, 1)

                def tile(i, q, t, peeled):
                    u = q * T + t
                    n = i * (2 * T) + u
                    v.wait_ge(tile_done, n + 1)
                    vv.tensor_tensor(wgt[:, t, :], pW[:, u % 2, 0:D], b2[:, :], ALU.add).then_inc(biased, 1)
                    v.wait_ge(biased, n + 1)
                    if t == 0:
                        v.wait_ge(small, i * 8 + (q * 4 + 4))
                    vv.scalar_tensor_tensor(msg[:, u, 0:D], pW[:, u % 2, D:2 * D], cut[:, q, t:t + 1],
                                            wgt[:, t, :], ALU.mult, ALU.mult).then_inc(msg_done, 1)

                def turn(i, q, ahead1, peeled):
                    slots(i, q, peeled)
                    if ahead1:
                        find_ends(i + q, 1 - q, peeled and q == 0)
                    for t in range(T):
                        tile(i, q, t, peeled)
                        if ahead1 and t == 2:
                            hidden(i * 2 + (q + 1), 1 - q)

                find_ends(0, 0, True)
                hidden(0, 0)
                v.wait_ge(fill_out, 16)
                for q in range(2):
                    turn(0, q, True, True)
                with v.Fori(1, G // 2 - 1) as i:
                    for q in range(2):
                        turn(i, q, True, False)
                for q in range(2):
                    turn(G // 2 - 1, q, q == 0, False)


def sum_phase(nc, io, S, keep):
    U = D_UNROLL
    accT = keep["accT"]
    with ExitStack() as ctx:
        sb, ps, sem = scope(nc, ctx)
        start, blk, first = keep["sched"][1]
        msg = sb("d_msg", [P, U, 2, MSG])
        local = sb("d_local", [P, U, 2])
        mask0 = sb("d_mask0", [P, U, P])
        mask1 = sb("d_mask1", [P, U, P])
        pD = ps("pD", [P, U, 512])
        zeroed = sem("d_zeroed")
        msg_in = [sem(f"d_msg_in{u}") for u in range(U)]
        local_done = sem("d_local_done")
        mask0_done = sem("d_mask0_done")
        mask1_done = sem("d_mask1_done")
        pool_passed = sem("d_pool_passed")
        mult = sem("d_mult")
        added = sem("d_added")
        ITER = TILES_S // U

        with nc.Block() as block:
            @block.sync
            def _(sp):
                def body(i, peeled):
                    at = registers(nc, sp, start[0:1, bass.ds(i * U, U)], U, E)
                    for u in range(U):
                        if not peeled:
                            sp.wait_ge(mult, i * U + (u + 1 - U))
                        sp.dma_start(msg[:, u, :, :].rearrange("p j m -> p (j m)"),
                                     S["messages"][bass.ds(at[u], PAIR), :].rearrange("(p j) m -> p (j m)", j=2)
                                     ).then_inc(msg_in[u], 16)

                body(0, True)
                with sp.Fori(1, ITER) as i:
                    body(i, False)

            @block.gpsimd
            def _(pool):
                def mask(i, u, peeled):
                    pool.wait_ge(local_done, i * U + (u + 1))
                    if not peeled:
                        pool.wait_ge(mult, i * U + (u + 1 - U))
                    passed(pool, pool_passed)
                    nc.gpsimd.tensor_scalar(mask1[:, u, :], keep["iota_row"][:, :], local[:, u, 1:2],
                                            None, ALU.is_equal).then_inc(mask1_done, 1)

                mid = NBLK // 2
                nc.gpsimd.memset(accT[:, mid:NBLK, :, :], 0.0).then_inc(zeroed, 1)
                for u in range(U):
                    mask(0, u, True)
                with pool.Fori(1, ITER) as i:
                    for u in range(U):
                        mask(i, u, False)

            @block.tensor
            def _(pe):
                def pair(i, u, peeled):
                    pe.wait_ge(msg_in[u], i * 16 + 16)
                    pe.wait_ge(mask0_done, i * U + (u + 1))
                    pe.wait_ge(mask1_done, i * U + (u + 1))
                    if not peeled:
                        pe.wait_ge(added, i * U + (u + 1 - U))
                    for k in range(DK):
                        for j in range(2):
                            ins = nc.tensor.matmul(pD[:, u, k * P:(k + 1) * P], msg[:, u, j, k * P:(k + 1) * P],
                                                   (mask0, mask1)[j][:, u, :], start=(j == 0), stop=(j == 1))
                    ins.then_inc(mult, 1)

                for u in range(U):
                    pair(0, u, True)
                with pe.Fori(1, ITER) as i:
                    for u in range(U):
                        pair(i, u, False)

            @block.vector
            def _(v):
                vv = nc.vector

                def locals_(i, u, peeled):
                    v.wait_ge(msg_in[u], i * 16 + 16)
                    vv.tensor_scalar(local[:, u, :], msg[:, u, :, D], first[:, bass.ds(i * U + u, 1)], None,
                                     ALU.subtract).then_inc(local_done, 1)

                def masks(i, u):
                    v.wait_ge(local_done, i * U + (u + 1))
                    vv.tensor_scalar(mask0[:, u, :], keep["iota_row"][:, :], local[:, u, 0:1],
                                     None, ALU.is_equal).then_inc(mask0_done, 1)

                def add(i, u, at, peeled):
                    v.wait_ge(mult, i * U + (u + 1))
                    if not (peeled and u == 0):
                        v.wait_ge(added, i * U + u)
                    to = accT[:, bass.ds(at, 1), :, :].rearrange("p a k n -> p (a k n)")
                    vv.tensor_tensor(to, pD[:, u, 0:D], to, ALU.add).then_inc(added, 1)

                vv.memset(accT[:, 0:NBLK // 2, :, :], 0.0).then_inc(zeroed, 1)
                v.wait_ge(zeroed, 2)
                for u in range(U):
                    locals_(0, u, True)
                    masks(0, u)

                def body(i, ahead, peeled):
                    at = registers(nc, v, blk[0:1, bass.ds(i * U, U)], U, NBLK - 1)
                    for u in range(U):
                        add(i, u, at[u], peeled)
                        if ahead:
                            if u:
                                masks(i + 1, u - 1)
                            locals_(i + 1, u, False)
                    if ahead:
                        masks(i + 1, U - 1)

                body(0, True, True)
                with v.Fori(1, ITER - 1) as i:
                    body(i, True, False)
                body(ITER - 1, False, False)


def output_phase(nc, io, S, keep):
    x1, accT = keep["acc"], keep["accT"]
    with ExitStack() as ctx:
        sb, ps, sem = scope(nc, ctx)
        lin2, bias = keep["lin2"], keep["lin2_b"]
        aggT = sb("e_aggT", [P, BU, DK, P])
        z = sb("e_z", [P, BU, D])
        soft = sb("e_soft", [P, BU, D])
        h = sb("e_h", [P, BU, D])
        stats = sb("e_stats", [P, BU, 6])
        mv = sb("e_mv", [P, BU, 2])
        logv = sb("e_logv", [P, BU])
        rstd = sb("e_rstd", [P, BU])
        newton = sb("e_newton", [P, BU])
        scale = sb("e_scale", [P, BU])
        eps = sb("e_eps", [P, 1])
        half_one = sb("e_half_one", [P, 1])
        out = sb("e_out", [P, BU, D])
        pE = ps("pE", [P, BU, 512])
        consts = sem("e_consts")
        staged = sem("e_staged")
        mult = sem("e_mult")
        z_done = sem("e_z_done")
        soft_step = sem("e_soft_step")
        v_passed = sem("e_v_passed")
        dve = sem("e_dve")
        h_done = sem("e_h_done")
        var_done = sem("e_var_done")
        log_done = sem("e_log_done")
        rstd_done = sem("e_rstd_done")
        out_done = sem("e_out_done")
        stored = [sem(f"e_stored{j}") for j in range(BU)]

        def at(a, b):
            return a[:, bass.ds(b, 1), :].rearrange("p a n -> p (a n)")

        with nc.Block() as block:
            @block.sync
            def _(sp):
                with sp.Fori(0, BI - 1) as i:
                    for j in range(BU):
                        sp.wait_ge(out_done, i * BU + (j + 1))
                        sp.dma_start(io["out"][bass.ds((i * BU + j) * P, P), :], out[:, j, :]).then_inc(stored[j], 16)
                for j in range(BU):
                    b = (BI - 1) * BU + j
                    rows = min(P, N - b * P)
                    sp.wait_ge(out_done, b + 1)
                    sp.dma_start(io["out"][b * P:b * P + rows, :], out[0:rows, j, :]).then_inc(stored[j], 16)
                for j in range(BU):
                    sp.wait_ge(stored[j], 16 * BI)

            @block.gpsimd
            def _(pool):
                g = nc.gpsimd
                g.memset(eps[:, :], 1e-5).then_inc(consts, 1)
                g.memset(half_one[:, :], 0.5).then_inc(consts, 1)

                def stage(i, j, peeled):
                    if not peeled:
                        pool.wait_ge(mult, i * BU + (j + 1 - BU))
                    g.tensor_copy(aggT[:, j, :, :].rearrange("p k n -> p (k n)"),
                                  accT[:, bass.ds(i * BU + j, 1), :, :].rearrange("p a k n -> p (a k n)")).then_inc(staged, 1)

                for j in range(BU):
                    stage(0, j, True)
                with pool.Fori(1, BI) as i:
                    for j in range(BU):
                        stage(i, j, False)

            @block.tensor
            def _(pe):
                def block_of(i, j, peeled):
                    pe.wait_ge(staged, i * BU + (j + 1))
                    if not peeled:
                        pe.wait_ge(z_done, i * BU + (j + 1 - BU))
                    for k in range(DK):
                        ins = nc.tensor.matmul(pE[:, j, 0:D], aggT[:, j, k, :], lin2[:, k, :],
                                               start=(k == 0), stop=(k == DK - 1))
                    ins.then_inc(mult, 1)

                for j in range(BU):
                    block_of(0, j, True)
                with pe.Fori(1, BI) as i:
                    for j in range(BU):
                        block_of(i, j, False)

            @block.scalar
            def _(act):
                def block_of(i, j, peeled):
                    n = i * BU + j
                    act.wait_ge(z_done, n + 1)
                    if not peeled:
                        act.wait_ge(h_done, i * BU + (j + 1 - BU))
                    nc.scalar.activation(soft[:, j, :], z[:, j, :], ACT.Abs).then_inc(soft_step, 1)
                    act.wait_ge(soft_step, n * 3 + 1)
                    nc.scalar.activation(soft[:, j, :], soft[:, j, :], ACT.Exp, scale=-1.0).then_inc(soft_step, 1)
                    act.wait_ge(soft_step, n * 3 + 2)
                    nc.scalar.activation(soft[:, j, :], soft[:, j, :], ACT.Ln, scale=0.5, bias=half_one[:, :]).then_inc(soft_step, 1)

                def deviations(i):
                    act.wait_ge(var_done, i + 1)
                    nc.scalar.activation(logv[:, :], mv[:, :, 1], ACT.Ln, bias=eps[:, :]).then_inc(log_done, 1)
                    act.wait_ge(log_done, i + 1)
                    nc.scalar.activation(rstd[:, :], logv[:, :], ACT.Exp, scale=-0.5).then_inc(rstd_done, 1)

                nc.scalar.preload_act_table_set("natural_log_exp_and_others")
                act.wait_ge(consts, 2)
                for j in range(BU):
                    block_of(0, j, True)
                with act.Fori(1, BI) as i:
                    for j in range(BU):
                        if j == BU - 2:
                            deviations(i - 1)
                        block_of(i, j, False)
                deviations(BI - 1)

            @block.vector
            def _(v):
                vv = nc.vector
                s = Steps(v, dve)

                def bias_of(i, j, peeled):
                    v.wait_ge(mult, i * BU + (j + 1))
                    if not peeled:
                        v.wait_ge(h_done, i * BU + (j + 1 - BU))
                    vv.tensor_tensor(z[:, j, :], pE[:, j, 0:D], bias[:, :], ALU.add).then_inc(z_done, 1)

                def sums(i, ahead, peeled):
                    n = s.n
                    for j in range(BU):
                        v.wait_ge(soft_step, i * (3 * BU) + (3 * j + 3))
                        if not peeled:
                            v.wait_ge(out_done, i * BU + (j + 1 - BU))
                        vv.scalar_tensor_tensor(h[:, j, :], z[:, j, :], 0.0, soft[:, j, :], ALU.max, ALU.add).then_inc(h_done, 1)
                        if ahead and j:
                            bias_of(i + 1, j - 1, False)
                    if ahead:
                        bias_of(i + 1, BU - 1, False)
                    for j in range(BU):
                        v.wait_ge(h_done, i * BU + (j + 1))
                        s.add(vv.scalar_tensor_tensor(h[:, j, :], at(x1, i * BU + j), 2.0, h[:, j, :], ALU.mult, ALU.add))
                    s.wait()
                    passed(v, v_passed)
                    for j in range(BU):
                        s.add(vv.bn_stats(stats[:, j, :], h[:, j, :]))
                    s.wait()
                    passed(v, v_passed)
                    for j in range(BU):
                        ins = vv.bn_aggr(mv[:, j, :], stats[:, j, :])
                    ins.then_inc(var_done, 1)

                def norm(i, peeled):
                    v.wait_ge(rstd_done, i + 1)
                    s.add(vv.tensor_tensor(newton[:, :], rstd[:, :], rstd[:, :], ALU.mult))
                    s.wait()
                    s.add(vv.scalar_tensor_tensor(newton[:, :], mv[:, :, 1], 1e-5, newton[:, :], ALU.add, ALU.mult))
                    s.wait()
                    s.add(vv.tensor_scalar(newton[:, :], newton[:, :], -0.5, 1.5, ALU.mult, ALU.add))
                    s.wait()
                    s.add(vv.tensor_tensor(scale[:, :], rstd[:, :], newton[:, :], ALU.mult))
                    s.wait()
                    for j in range(BU):
                        if not peeled:
                            v.wait_ge(stored[j], i * 16)
                        vv.tensor_scalar(out[:, j, :], h[:, j, :], mv[:, j, 0:1], scale[:, j:j + 1],
                                         ALU.subtract, ALU.mult).then_inc(out_done, 1)

                for j in range(BU):
                    bias_of(0, j, True)
                sums(0, True, True)
                norm(0, True)
                with v.Fori(1, BI - 1) as i:
                    s.loop(i, 1, 2 * BU + 4)
                    sums(i, True, False)
                    norm(i, False)
                s.end(BI - 2)
                sums(BI - 1, False, False)
                norm(BI - 1, False)


def gnn_kernel(nc, io):
    with ExitStack() as ctx:
        sb, ps, sem = scope(nc, ctx)
        S = dict(
            table=nc.dram_tensor("table", [NBLK * P * REL, D], F32).ap(),
            records=nc.dram_tensor("records", [EP, META], F32).ap(),
            attr50=nc.dram_tensor("sorted_attr50", [EP, G50], F32).ap(),
            start=nc.dram_tensor("tile_start", [2, CD * P], I32).ap(),
            block=nc.dram_tensor("tile_block", [2, CD * P], I32).ap(),
            first_node=nc.dram_tensor("tile_first_node", [2, CD * P], F32).ap(),
            messages=nc.dram_tensor("messages", [E + PAIR, MSG], F32).ap())
        keep = dict(acc=sb("acc", [P, NBLK, D]), ident=sb("ident", [P, P]), iota_row=sb("iota_row", [P, P]))
        keep["sched"] = [(sb(f"start_{k}", [1, cols * P], I32), sb(f"block_{k}", [1, cols * P], I32),
                          sb(f"first_{k}", [P, cols * P])) for k, cols in enumerate((CD, CS))]
        setup_phase(nc, io, S, keep)
        for name in ("lin1", "lin2", "w2"):
            keep[name] = sb(f"k_{name}", [P, DK, D])
        for name in ("h_bias", "b2", "lin2_b"):
            keep[name] = sb(f"k_{name}", [P, D])
        keep["w1"] = sb("k_w1", [P, P])
        relation_phase(nc, io, S, keep)
        with nc.sbuf_tensor("y3", [P, NBLK, 3, D], BF16) as keep["y3"]:
            norm_phase(nc, io, S, keep)
            edge_phase(nc, io, S, keep)
        with nc.sbuf_tensor("accT", [P, NBLK, DK, P], F32) as keep["accT"]:
            sum_phase(nc, io, S, keep)
            output_phase(nc, io, S, keep)


def host_arrays(x, src, dst, edge_attr_3, edge_attr_50, edge_type_16, edge_weight1, L0_gnn_weight,
                L0_gnn_w_comp, L0_gnn_h_bias, L0_gnn_loop_weight, L1_gnn_mlp_w1, L1_gnn_mlp_b1,
                L1_gnn_mlp_w2, L1_gnn_mlp_b2, L1_gnn_lin1_w, L1_gnn_lin2_w, L1_gnn_lin2_b):
    import numpy as np

    def pad(a, rows, fill=0):
        a = np.asarray(a)
        out = np.full((rows,) + a.shape[1:], fill, a.dtype)
        out[:a.shape[0]] = a
        return out

    xp = pad(x, NBLK * P)
    return dict(
        x=xp,
        xT=np.ascontiguousarray(xp.reshape(NBLK, P, DK, P).transpose(0, 3, 2, 1)).reshape(NBLK, P, DK * P),
        src=pad(src, EP, PADNODE).reshape(P, EC), dst=pad(dst, EP, PADNODE).reshape(P, EC),
        etype=pad(edge_type_16, EP).reshape(P, EC), norm=pad(edge_weight1, EP).reshape(P, EC),
        attr3=pad(edge_attr_3, EP).reshape(P, EC * 3), attr50=pad(edge_attr_50, EP),
        weight=np.asarray(L0_gnn_weight), w_comp=np.asarray(L0_gnn_w_comp).reshape(1, REL * BASES),
        h_bias=np.asarray(L0_gnn_h_bias).reshape(1, D), loop_weight=np.asarray(L0_gnn_loop_weight),
        w1=np.asarray(L1_gnn_mlp_w1), b1=np.asarray(L1_gnn_mlp_b1).reshape(1, D),
        w2=np.asarray(L1_gnn_mlp_w2), b2=np.asarray(L1_gnn_mlp_b2).reshape(1, D),
        lin1=np.asarray(L1_gnn_lin1_w), lin2=np.asarray(L1_gnn_lin2_w),
        lin2_b=np.asarray(L1_gnn_lin2_b).reshape(1, D))


def kernel(**inputs):
    import numpy as np
    import concourse.bacc as bacc
    from concourse.bass_utils import run_bass_kernel_spmd

    nc = bacc.Bacc("TRN2", target_bir_lowering=False, num_devices=1)
    arrays = {f"in_{name}_dram": a for name, a in host_arrays(**inputs).items()}
    io = {name[3:-5]: nc.dram_tensor(name, a.shape, mybir.dt.from_np(a.dtype), kind="ExternalInput").ap()
          for name, a in arrays.items()}
    io["out"] = nc.dram_tensor("out_0_dram", (N, D), F32, kind="ExternalOutput").ap()
    gnn_kernel(nc, io)
    r = run_bass_kernel_spmd(nc, [arrays], core_ids=[0])
    return np.asarray(r.results[0]["out_0_dram"])
```
